# Optimizing a Trainium2 kernel written in Bass

```python
import numpy as np
import jax
import jax.numpy as jnp

def _softmax(x, axis=-1):
    return jax.nn.softmax(x, axis=axis)

def _gelu(x):
    return jax.nn.gelu(x, approximate=True)

def _silu(x):
    return jax.nn.silu(x)

def _sigmoid(x):
    return jax.nn.sigmoid(x)

def _layernorm(x, axis=-1, eps=1e-05):
    m = jnp.mean(x, axis=axis, keepdims=True)
    v = jnp.var(x, axis=axis, keepdims=True)
    return (x - m) / jnp.sqrt(v + eps)

def _scatter_add(tgt, idx, src, axis=0):
    return tgt.at[idx].add(src)

def _segment_sum(src, seg, n):
    return jax.ops.segment_sum(src, seg, n)
kernel_name = 'mk_hybrid_d1_jaxref_r8_4b864a'

def setup_inputs(seed: int=0):
    np.random.seed(seed)
    _w = jnp.asarray

    def _L0_attn_a_setup():
        import math
        import jax, jax.numpy as jnp
        import numpy as np
        NUM_HEADS = 16
        NUM_BUCKETS = 32

        def _relative_position_bucket(relative_position):
            num_buckets = NUM_BUCKETS
            n = jnp.maximum(-relative_position, 0)
            max_exact = num_buckets // 2
            is_small = n < max_exact
            n_safe = jnp.maximum(n, 1).astype(jnp.float32)
            val_if_large = max_exact + (jnp.log(n_safe / max_exact) / math.log(num_buckets / max_exact) * (num_buckets - max_exact)).astype(jnp.int32)
            val_if_large = jnp.minimum(val_if_large, num_buckets - 1)
            return jnp.where(is_small, n, val_if_large)
        key = jax.random.key(seed)
        ks = jax.random.split(key, 8)
        B, S, D = (2, 256, 128)
        s = 1.0 / math.sqrt(D)
        return {'hidden_states': jax.random.normal(ks[0], (B, S, D), jnp.float32), 'Wq': jax.random.normal(ks[1], (D, D), jnp.float32) * s, 'bq': jnp.zeros((D,), jnp.float32), 'Wk': jax.random.normal(ks[2], (D, D), jnp.float32) * s, 'bk': jnp.zeros((D,), jnp.float32), 'Wv': jax.random.normal(ks[3], (D, D), jnp.float32) * s, 'bv': jnp.zeros((D,), jnp.float32), 'rel_bias': jax.random.normal(ks[4], (NUM_BUCKETS, NUM_HEADS), jnp.float32) * 0.02}
    _L0_attn_a_in = _L0_attn_a_setup()

    def _L0_attn_b_setup():
        import jax, jax.numpy as jnp
        import numpy as np
        NUM_HEADS = 16
        SCALE = (128 // NUM_HEADS) ** (-0.5)
        key = jax.random.key(seed)
        k1, k2, k3, k4, k5 = jax.random.split(key, 5)
        L, N, E, inner = (256, 4, 128, 128)
        return {'query': jax.random.normal(k1, (L, N, E), dtype=jnp.float32), 'qkv_proj': jax.random.normal(k2, (3 * inner, E), dtype=jnp.float32) * 0.02, 'qkv_bias': jax.random.normal(k3, (3 * inner,), dtype=jnp.float32) * 0.02, 'out_proj': jax.random.normal(k4, (E, inner), dtype=jnp.float32) * 0.02, 'out_bias': jax.random.normal(k5, (E,), dtype=jnp.float32) * 0.02}
    _L0_attn_b_in = _L0_attn_b_setup()

    def _L0_ffn_setup():
        import jax, jax.numpy as jnp
        import numpy as np
        H, I, E_ROUTED, TOP_K = (128, 352, 7, 2)
        B, S = (4, 256)

        def _expert(h, g, u, d):
            return jnp.einsum('...i,hi->...h', jax.nn.silu(h @ g.T) * (h @ u.T), d)
        key = jax.random.key(seed)
        ks = jax.random.split(key, 10)
        sc = 0.02
        return {'x': jax.random.normal(ks[0], (B, S, H), dtype=jnp.float32), 'sg': jax.random.normal(ks[1], (I, H), dtype=jnp.float32) * sc, 'su': jax.random.normal(ks[2], (I, H), dtype=jnp.float32) * sc, 'sd': jax.random.normal(ks[3], (H, I), dtype=jnp.float32) * sc, 'rg': jax.random.normal(ks[4], (E_ROUTED, I, H), dtype=jnp.float32) * sc, 'ru': jax.random.normal(ks[5], (E_ROUTED, I, H), dtype=jnp.float32) * sc, 'rd': jax.random.normal(ks[6], (E_ROUTED, H, I), dtype=jnp.float32) * sc, 'wr': jax.random.normal(ks[7], (E_ROUTED, H), dtype=jnp.float32) * sc, 'rb': jnp.zeros((E_ROUTED,), dtype=jnp.float32)}
    _L0_ffn_in = _L0_ffn_setup()
    _d = {'L0_attn_a_hidden_states': _L0_attn_a_in['hidden_states'], 'L0_attn_a_Wq': _L0_attn_a_in['Wq'], 'L0_attn_a_bq': _L0_attn_a_in['bq'], 'L0_attn_a_Wk': _L0_attn_a_in['Wk'], 'L0_attn_a_bk': _L0_attn_a_in['bk'], 'L0_attn_a_Wv': _L0_attn_a_in['Wv'], 'L0_attn_a_bv': _L0_attn_a_in['bv'], 'L0_attn_a_rel_bias': _L0_attn_a_in['rel_bias'], 'L0_attn_b_qkv_proj': _L0_attn_b_in['qkv_proj'], 'L0_attn_b_qkv_bias': _L0_attn_b_in['qkv_bias'], 'L0_attn_b_out_proj': _L0_attn_b_in['out_proj'], 'L0_attn_b_out_bias': _L0_attn_b_in['out_bias'], 'L0_ffn_sg': _L0_ffn_in['sg'], 'L0_ffn_su': _L0_ffn_in['su'], 'L0_ffn_sd': _L0_ffn_in['sd'], 'L0_ffn_rg': _L0_ffn_in['rg'], 'L0_ffn_ru': _L0_ffn_in['ru'], 'L0_ffn_rd': _L0_ffn_in['rd'], 'L0_ffn_wr': _L0_ffn_in['wr'], 'L0_ffn_rb': _L0_ffn_in['rb']}
    _x0 = _d['L0_attn_a_hidden_states']
    _d['L0_attn_a_hidden_states'] = jax.random.normal(jax.random.fold_in(jax.random.key(seed), 1), (32, 256, 128), dtype=_x0.dtype)
    del _x0
    return _d

def reference(L0_attn_a_hidden_states, L0_attn_a_Wq, L0_attn_a_bq, L0_attn_a_Wk, L0_attn_a_bk, L0_attn_a_Wv, L0_attn_a_bv, L0_attn_a_rel_bias, L0_attn_b_qkv_proj, L0_attn_b_qkv_bias, L0_attn_b_out_proj, L0_attn_b_out_bias, L0_ffn_sg, L0_ffn_su, L0_ffn_sd, L0_ffn_rg, L0_ffn_ru, L0_ffn_rd, L0_ffn_wr, L0_ffn_rb):

    def _L0_attn_a_ref(hidden_states, Wq, bq, Wk, bk, Wv, bv, rel_bias):
        import math
        import jax, jax.numpy as jnp
        import numpy as np
        NUM_HEADS = 16
        NUM_BUCKETS = 32

        def _relative_position_bucket(relative_position):
            num_buckets = NUM_BUCKETS
            n = jnp.maximum(-relative_position, 0)
            max_exact = num_buckets // 2
            is_small = n < max_exact
            n_safe = jnp.maximum(n, 1).astype(jnp.float32)
            val_if_large = max_exact + (jnp.log(n_safe / max_exact) / math.log(num_buckets / max_exact) * (num_buckets - max_exact)).astype(jnp.int32)
            val_if_large = jnp.minimum(val_if_large, num_buckets - 1)
            return jnp.where(is_small, n, val_if_large)
        B, S, D = hidden_states.shape
        H = NUM_HEADS
        dh = D // H
        q = (hidden_states @ Wq + bq).reshape(B, S, H, dh)
        k = (hidden_states @ Wk + bk).reshape(B, S, H, dh)
        v = (hidden_states @ Wv + bv).reshape(B, S, H, dh)
        scores = jnp.einsum('bqhd,bkhd->bhqk', q, k) / math.sqrt(dh)
        ctx_pos = jnp.arange(S)[:, None]
        mem_pos = jnp.arange(S)[None, :]
        buckets = _relative_position_bucket(mem_pos - ctx_pos)
        bias = rel_bias[buckets]
        bias = jnp.transpose(bias, (2, 0, 1))
        scores = scores + bias[None]
        attn = jax.nn.softmax(scores, axis=-1)
        context = jnp.einsum('bhqk,bkhd->bqhd', attn, v).reshape(B, S, D)
        return context

    def _L0_attn_b_ref(query, qkv_proj, qkv_bias, out_proj, out_bias):
        import jax, jax.numpy as jnp
        import numpy as np
        NUM_HEADS = 16
        SCALE = (128 // NUM_HEADS) ** (-0.5)
        L, N, E = query.shape
        h = NUM_HEADS
        inner = qkv_proj.shape[0] // 3
        d = inner // h
        qkv = jnp.einsum('lne,fe->lnf', query, qkv_proj) + qkv_bias
        qkv = qkv.reshape(L, N, inner, 3)
        q, k, v = (qkv[..., 0], qkv[..., 1], qkv[..., 2])
        q = q.reshape(L, N * h, d).transpose(1, 0, 2)
        k = k.reshape(L, N * h, d).transpose(1, 0, 2)
        v = v.reshape(L, N * h, d).transpose(1, 0, 2)
        attn = SCALE * jnp.einsum('bld,bmd->blm', q, k)
        attn = jax.nn.softmax(attn, axis=-1)
        out = jnp.einsum('blm,bmd->bld', attn, v)
        out = out.transpose(1, 0, 2).reshape(L, N, inner)
        out = jnp.einsum('lni,ei->lne', out, out_proj) + out_bias
        return out

    def _L0_ffn_ref(x, sg, su, sd, rg, ru, rd, wr, rb):
        import jax, jax.numpy as jnp
        import numpy as np
        H, I, E_ROUTED, TOP_K = (128, 352, 7, 2)
        B, S = (4, 256)

        def _expert(h, g, u, d):
            return jnp.einsum('...i,hi->...h', jax.nn.silu(h @ g.T) * (h @ u.T), d)
        shared_out = _expert(x, sg, su, sd)
        logits = x @ wr.T + rb
        probs = jax.nn.softmax(logits, axis=-1)
        scores, idx = jax.lax.top_k(probs, TOP_K)
        scores = scores / scores.sum(axis=-1, keepdims=True)
        w = jnp.sum(scores[..., None] * jax.nn.one_hot(idx, E_ROUTED, dtype=x.dtype), axis=-2)
        out = shared_out
        for e in range(E_ROUTED):
            out = out + w[..., e:e + 1] * _expert(x, rg[e], ru[e], rd[e])
        return out
    x = L0_attn_a_hidden_states
    x = x + _L0_attn_a_ref(_layernorm(x, axis=-1), L0_attn_a_Wq, L0_attn_a_bq, L0_attn_a_Wk, L0_attn_a_bk, L0_attn_a_Wv, L0_attn_a_bv, L0_attn_a_rel_bias)
    x = x + _L0_ffn_ref(_layernorm(x, axis=-1), L0_ffn_sg, L0_ffn_su, L0_ffn_sd, L0_ffn_rg, L0_ffn_ru, L0_ffn_rd, L0_ffn_wr, L0_ffn_rb)
    x = x + _L0_attn_b_ref(_layernorm(x, axis=-1), L0_attn_b_qkv_proj, L0_attn_b_qkv_bias, L0_attn_b_out_proj, L0_attn_b_out_bias)
    x = x + _L0_ffn_ref(_layernorm(x, axis=-1), L0_ffn_sg, L0_ffn_su, L0_ffn_sd, L0_ffn_rg, L0_ffn_ru, L0_ffn_rd, L0_ffn_wr, L0_ffn_rb)
    return x

_drawn_inputs = setup_inputs


def setup_inputs(seed=0):
    import zlib

    import numpy as np

    out = dict(_drawn_inputs(seed))
    spreads = {'L0_attn_a_bq': (0.0, 0.57),
     'L0_attn_a_bk': (0.0, 0.8),
     'L0_attn_a_bv': (0.0, 0.1),
     'L0_ffn_rb': (0.0, 0.8)}
    factors = {'L0_attn_a_rel_bias': 8.0,
     'L0_attn_b_qkv_proj': 5.365,
     'L0_attn_b_qkv_bias': 8.0,
     'L0_attn_b_out_proj': 4.735,
     'L0_attn_b_out_bias': 2.811,
     'L0_ffn_sg': 2.92,
     'L0_ffn_su': 2.856,
     'L0_ffn_sd': 2.875,
     'L0_ffn_rg': 4.191,
     'L0_ffn_ru': 4.17,
     'L0_ffn_rd': 4.162,
     'L0_ffn_wr': 5.096}
    for name, (base, spread) in spreads.items():
        noise = np.random.default_rng([zlib.crc32(name.encode()), seed]).standard_normal(out[name].shape)
        drawn = base * np.exp(spread * noise) if base else spread * noise
        out[name] = jnp.asarray(drawn.astype(out[name].dtype))
    for name, factor in factors.items():
        out[name] = (out[name] * factor).astype(out[name].dtype)
    return out
```

```python
import numpy as np
import concourse.bass as bass
from concourse import mybir

F32 = mybir.dt.float32
F32R = mybir.dt.float32r
I32 = mybir.dt.int32
U32 = mybir.dt.uint32
ALU = mybir.AluOpType
ACT = mybir.ActivationFunctionType
AX = mybir.AxisListType

P = 128
BATCH, SEQ, D = 32, 256, 128
HEADS, DH = 16, 8
BUCKETS = 32
EXPERTS, INNER = 8, 352
TILES_I = 3
CHUNK = 512
TOK = CHUNK // P
PASSES = BATCH * SEQ // CHUNK
POS = CHUNK // BATCH
GROUPS = HEADS // 4
UNITS = 2 * HEADS
FT = EXPERTS * TILES_I
EPS = 1e-5
MAGIC = float(0x5F3759DF)
NEWTON = 3
FAR = 3.0e38

CREDIT = 8

Z_RING = 4
PT_RING = 5
NM_RING = 8
H_RING = 2
CUT_RING = 3
DOWN_LAG = 2

VW = DH + 1
STAGE, PIECES = 1536, 3
SCALE = float(DH) ** -0.5

USES = {"A": {"S0": 20, "S1": 20, "T": 5 + UNITS, "O": 2 * 2 * GROUPS},
        "B": {"S0": 6, "S1": 5, "T": 7, "O": 1 + TOK}}

C_ID, C_MQ, C_MK, C_IOTA, C_HOT, C_SEL = 0, 128, 129, 130, 138, 650
C_FLIP = C_SEL + 7 * 128
C_KEPT = C_HOT
C_ALL = C_FLIP + P


def constants():
    c = np.zeros((P, C_ALL), np.float32)
    c[:, C_ID:C_ID + P] = np.eye(P)
    row = np.arange(P) % 32 // 8
    c[:, C_MQ] = np.where(row >= 2, -1.0, 0.0)
    c[:, C_MK] = np.where(row % 2 == 1, -1.0, 0.0)
    c[:, C_IOTA:C_IOTA + 8] = np.arange(8)
    exact = BUCKETS // 2
    for x in range(2 * SEQ - 1):
        n = max(SEQ - 1 - x, 0)
        if n < exact:
            b = n
        else:
            ratio = np.log(np.float32(n) / np.float32(exact)) / np.float32(np.log(BUCKETS / exact))
            b = min(exact + int(ratio * np.float32(BUCKETS - exact)), BUCKETS - 1)
        c[b, C_HOT + x] = 1.0
    for e in range(7):
        c[e, C_SEL + e * P:C_SEL + (e + 1) * P] = 1.0
        c[8 + e, C_SEL + e * P:C_SEL + (e + 1) * P] = 1.0
    c[:, C_FLIP:C_FLIP + P] = np.eye(P)[::-1]
    return c


class Pass:

    def __init__(self, kind, i):
        self.kind, self.i = kind, i
        self.g = i if kind == "A" else i + PASSES

    def count(self, per, n):
        before = 0 if self.kind == "A" else PASSES * per["A"]
        return self.i * per[self.kind] + (CREDIT + before + n)


def same(n):
    return {"A": n, "B": n}


def steps_attention(kind):
    out = [("load", 0, 0.1), ("norm1", 0, 4.0), ("turn1", 0, 1.0)]
    out += [("qk", n, 1.0) for n in range(2 * GROUPS)] + [("v", 0, 1.0)]
    if kind == "A":
        for u in range(UNITS + 8):
            if u < UNITS:
                out.append(("scores", u, 1.0))
            if 2 <= u < UNITS + 2:
                out.append(("probs", u - 2, 1.0))
            if u >= 6 and (u - 6) % 4 == 0 and (u - 6) // 4 < 8:
                out.append(("mix", (u - 6) // 4, 1.0))
            if u >= 8 and (u - 8) % 4 == 0 and (u - 8) // 4 < 8:
                out.append(("context", (u - 8) // 4, 0.8))
    else:
        for r in range(5):
            if r < 4:
                out.append(("bscores", r, 3.0))
            if r >= 1:
                out.append(("bprobs", r - 1, 1.0))
        out += [("bmix", t, 3.0) for t in range(TOK)] + [("bturn", 0, 1.5), ("bout", 0, 2.0)]
    return out + [("norm2", 0, 4.0), ("turn2", 0, 1.0), ("logits", 0, 2.0), ("route", 0, 3.0), ("wturn", 0, 1.0)]


def steps_experts():
    out = [("begin", 0, 1.0)]
    for i in range(FT + DOWN_LAG + 1):
        if i < FT:
            out.append(("up", i, 1.0))
            out.append(("gate", i, 0.3))
        if 1 <= i <= FT:
            out.append(("cut", i - 1, 0.3))
        if DOWN_LAG <= i < FT + DOWN_LAG:
            n = i - DOWN_LAG
            out.append(("down", n, 1.0))
            if n % TILES_I == TILES_I - 1:
                out.append(("add", n // TILES_I, 0.3))
                if n < FT - 1:
                    out.append(("weight", n // TILES_I + 1, 0.3))
    return out + [("end", 0, 1.0)]


def merged(a, f):
    ta, tf = sum(s[2] for s in a) or 1.0, sum(s[2] for s in f) or 1.0
    out, ca, cf, na, nf = [], 0.0, 0.0, 0, 0
    while na < len(a) or nf < len(f):
        if nf < len(f) and (na == len(a) or cf / tf <= ca / ta):
            out.append((True,) + f[nf][:2])
            cf += f[nf][2]
            nf += 1
        else:
            out.append((False,) + a[na][:2])
            ca += a[na][2]
            na += 1
    return out


ALONE = {k: [(False,) + s[:2] for s in steps_attention(k)] for k in "AB"}
EXPERTS_ALONE = [(True,) + s[:2] for s in steps_experts()]
BESIDE = {k: merged(steps_attention(k), steps_experts()) for k in "AB"}


def run_passes(engine, attention, experts):
    for kind in "AB":
        for _, step, n in ALONE[kind]:
            attention(Pass(kind, 0), step, n)
        with engine.Fori(0, PASSES - 1) as i:
            this, following = Pass(kind, i), Pass(kind, i + 1)
            for is_expert, step, n in BESIDE[kind]:
                if is_expert:
                    experts(this, step, n)
                else:
                    attention(following, step, n)
        for _, step, n in EXPERTS_ALONE:
            experts(Pass(kind, PASSES - 1), step, n)


def spread(ap, axis, n):
    ap = ap.unsqueeze(axis)
    shape = list(ap.shape)
    shape[axis] = n
    return ap.broadcast_to(shape)


def program(nc, x, wq, bq, wk, bk, wv, bv, rel, wqkv, bqkv, wo, bo, wg, wu, wd, wr, rb, const, out):
    def sb(name, shape, dt=F32):
        return nc.alloc_sbuf_tensor(name, shape, dt)

    cst = sb("cst", [P, C_KEPT])
    ident = cst[:, C_ID:C_ID + P]
    sel = sb("sel", [16, 7 * P], F32R)
    ones = sb("ones", [1, P])
    raw_b = sb("raw_b", [P, 2, P])
    proj = sb("proj", [P, 2, GROUPS * P])
    proj_v = sb("proj_v", [P, 2, P])
    proj_o = sb("proj_o", [P, P])
    bcol = sb("bcol", [P, 4 * GROUPS])
    bc = sb("bc", [P, 3 * P + 8])
    router = sb("router", [P, 8])
    w_hi = [sb(f"w{n}_hi", [P, EXPERTS * INNER], F32R) for n in "gu"]
    w_lo = [sb(f"w{n}_lo", [P, EXPERTS * INNER], F32R) for n in "gu"]
    wd_hi = sb("wd_hi", [P, FT, P], F32R)
    wd_lo = sb("wd_lo", [P, FT, P], F32R)
    big = sb("big", [P, HEADS * 3 * P])
    bias_a = big[:, :].rearrange("p (h y) -> p h y", h=HEADS)
    qb = big[:, 0:GROUPS * CHUNK].rearrange("p (g t) -> p g t", g=GROUPS)
    kb = big[:, GROUPS * CHUNK:2 * GROUPS * CHUNK].rearrange("p (g t) -> p g t", g=GROUPS)

    xin = sb("xin", [P, TOK, D])
    xn = sb("xn", [P, TOK, D])
    xnT = sb("xnT", [P, CHUNK])
    stats = sb("stats", [P, TOK, 6])
    moments = sb("moments", [P, TOK, 2])
    rs = sb("rs", [P, 4, TOK])
    shifted = sb("shifted", [P, 2, CHUNK])
    high = sb("high", [P, CHUNK], F32R)
    qx = sb("qx", [P, GROUPS, CHUNK], F32R)
    kx = sb("kx", [P, GROUPS, CHUNK], F32R)
    vx = sb("vx", [P, TOK, HEADS * VW + 32 - VW])
    z = sb("z", [P, Z_RING, 2 * SEQ])
    nm = sb("nm", [P, NM_RING, 2])
    probT = sb("probT", [P, PT_RING, 2 * SEQ])
    oT = sb("oT", [P, 2, SEQ])
    rec = sb("rec", [P, HEADS])
    ctxt = sb("ctxt", [P, 2, 4, DH])
    h1 = sb("h1", [P, TOK, D])
    xf = sb("xf", [P, CHUNK])
    lg = sb("lg", [P, TOK, 8])
    top = sb("top", [P, TOK, 8])
    at = sb("at", [P, TOK, 8], U32)
    atf = sb("atf", [P, TOK, 8])
    gap = sb("gap", [P, TOK])
    e2 = sb("e2", [P, TOK])
    share = sb("share", [P, 3, TOK])
    wtok = sb("wtok", [P, 3, TOK, 8])
    whi = sb("whi", [P, TOK, 8], F32R)
    wcat = sb("wcat", [P, TOK, 16])
    wts = sb("wts", [16, CHUNK])
    maxb = sb("maxb", [P, 4, HEADS])
    ctxb = xn
    ctxT = xnT
    B_BANKS = (("S0", GROUPS), ("S1", GROUPS), ("T", 2), ("O", 0))

    xh = sb("xh", [P, CHUNK], F32R)
    xl = sb("xl", [P, CHUNK], F32R)
    wTF = sb("wTF", [16, CHUNK], F32R)
    hid_hi = sb("hid_hi", [P, CUT_RING, CHUNK], F32R)
    hid_lo = sb("hid_lo", [P, CUT_RING, CHUNK], F32R)
    work = sb("work", [P, PIECES * STAGE])
    stage = work[:, :].rearrange("p (s c) -> p s c", s=PIECES)
    slot = work[:, :].rearrange("p (s c) -> p s c", c=CHUNK)
    th = slot[:, 0:2, :]
    hid = slot[:, 2:4, :]
    wbS, part, acc = slot[:, 4, :], slot[:, 5, :], slot[:, 6, :]
    h1F = slot[:, 7, :].rearrange("p (t d) -> p t d", t=TOK)
    xo = slot[:, 8, :].rearrange("p (t d) -> p t d", t=TOK)

    raw_a = z[:, 0, 0:2 * P].rearrange("p (m c) -> p m c", m=2)
    row_bc = z[0:1, 1, 0:3 * P + 8]
    trev = z[0:HEADS, 2, :]
    relb = z[0:BUCKETS, 3, 0:HEADS]
    row_raw = oT[0:1, :, :].rearrange("p a b -> p (a b)").rearrange("p (m c) -> p m c", m=4)
    row_rep = probT[0:1, 0:4, :]
    hot = stage[0:BUCKETS, 2, 0:512]
    sel_raw = stage[0:16, 2, 512:512 + 7 * P]
    flip = stage[:, 2, 512 + 7 * P:512 + 8 * P]

    BANKS = ("S0", "S1", "T", "O", "G", "U", "Y", "W")
    bank = {n: nc.alloc_psum_tensor(f"bank_{n}", [P, 512], F32) for n in BANKS}

    trev_dram = nc.dram_tensor("trev_dram", [HEADS, 512], F32).ap()
    x2 = nc.dram_tensor("x2", [BATCH * SEQ, D], F32).ap()

    sem = nc.alloc_semaphore
    w_landed, row_landed, rel_landed = sem("w_landed"), sem("row_landed"), sem("rel_landed")
    trev_stored, bias_landed = sem("trev_stored"), sem("bias_landed")
    flipped, bias_ready = sem("flipped"), sem("bias_ready")
    piece_landed = [sem(f"piece_landed_{k}") for k in range(2 * PIECES)]
    x_landed, stored = sem("x_landed"), sem("stored")
    setup_dve, setup_pe, proj_b_ready = sem("setup_dve"), sem("setup_pe"), sem("proj_b_ready")
    halved, high_cut, pieces_cut = sem("halved"), sem("high_cut"), sem("pieces_cut")
    filled = {n: sem(f"filled_{n}") for n in BANKS if n != "Y"}
    emptied = {n: sem(f"emptied_{n}") for n in ("S0", "S1", "T", "O", "W")}
    normed1, kept, qk_ready, exp_done = sem("normed1"), sem("kept"), sem("qk_ready"), sem("exp_done")
    turned, h1_part, normed2 = sem("turned"), sem("h1_part"), sem("normed2")
    gap_ready, e2_ready, wcat_ready, vstep = sem("gap_ready"), sem("e2_ready"), sem("wcat_ready"), sem("vstep")
    xh_ready, xl_ready, wTF_ready, h1F_ready = sem("xh_ready"), sem("xl_ready"), sem("wTF_ready"), sem("h1F_ready")
    th_ready, a_ready, h_ready = sem("th_ready"), sem("a_ready"), sem("h_ready")
    hh_ready, hl_ready, down_done = sem("hh_ready"), sem("hl_ready"), sem("down_done")
    combined, acc_ready = sem("combined"), sem("acc_ready")

    PASS_SCORES = {"A": UNITS, "B": TOK}

    def use(p, name, n):
        return p.count({k: USES[k][name] for k in "AB"}, n + 1)

    def landed(p):
        return (p.i + 1) * 16 if p.kind == "A" else (p.i + 1) * 64 + 16 * PASSES

    passed = {}

    def alone(eng):
        if eng not in passed:
            passed[eng] = sem(f"passed_{len(passed)}")
        eng.sem_inc(passed[eng], 1)

    def last_use(p, name, back=1):
        return USES[p.kind][name] - back

    def rows_of(i):
        return P if i % TILES_I < TILES_I - 1 else INNER - P * (TILES_I - 1)

    def cols_of(i):
        lo = (i // TILES_I) * INNER + (i % TILES_I) * P
        return slice(lo, lo + rows_of(i))

    def head_cols(ap, copies):
        return ap.rearrange("p (h r d) -> p h r d", h=HEADS, r=copies)

    def turned_out(eng, copy, p, n):
        eng.wait_ge(filled["T"], use(p, "T", 2 + n))
        eng.wait_ge(filled["O"], use(p, "O", 2 * ((n - PT_RING) // 4)))
        copy(probT[:, n % PT_RING, :], bank["T"][:, :]).then_inc(emptied["T"], 1)

    with nc.Block() as block:
        @block.sync
        def _(sp):
            sp.sem_inc(stored, 16)
            sp.dma_start(cst[:, :], const[:, 0:C_KEPT]).then_inc(w_landed, 16)
            sp.dma_start(hot, const[0:BUCKETS, C_HOT:C_HOT + 512]).then_inc(w_landed, 16)
            sp.dma_start(sel_raw, const[0:16, C_SEL:C_FLIP]).then_inc(w_landed, 16)
            sp.dma_start(flip, const[:, C_FLIP:C_ALL]).then_inc(w_landed, 16)
            sp.dma_start(relb, rel).then_inc(w_landed, 16)
            sp.dma_start(raw_a[:, 0, :], wq).then_inc(w_landed, 16)
            sp.dma_start(raw_a[:, 1, :], wk).then_inc(w_landed, 16)
            sp.dma_start(row_raw[:, 0, :], bq).then_inc(row_landed, 16)
            sp.dma_start(row_raw[:, 1, :], bk).then_inc(row_landed, 16)
            sp.dma_start(row_raw[:, 2:4, :], bqkv[:, 0:2, :]).then_inc(row_landed, 16)
            sp.wait_ge(setup_dve, 3)
            sp.dma_start(row_bc[:, 0:P], bv).then_inc(row_landed, 16)
            sp.dma_start(row_bc[:, P:2 * P], bqkv[:, 2, :]).then_inc(row_landed, 16)
            sp.dma_start(row_bc[:, 2 * P:3 * P], bo).then_inc(row_landed, 16)
            sp.dma_start(row_bc[:, 3 * P:3 * P + 7], rb).then_inc(row_landed, 16)
            sp.dma_start(router[:, 0:7], wr).then_inc(row_landed, 16)

            def load(p):
                sp.wait_ge(normed1, p.count(same(1), 0))
                sp.wait_ge(kept, p.count(same(1), 0))
                if p.kind == "A":
                    src = x[bass.ds(p.i * CHUNK, CHUNK), :].rearrange("(t p) d -> p t d", p=P)
                    sp.dma_start(xin[:, :, :], src).then_inc(x_landed, 16)
                    return
                if isinstance(p.i, int):
                    sp.wait_ge(stored, 16 * (PASSES + 1))
                for j in range(4):
                    sp.dma_start(xin[32 * j:32 * j + 32, :, :], positions(x2, p.i, j)).then_inc(x_landed, 16)

            def positions(rows, i, j):
                v = rows.rearrange("(l c t j) d -> j l c t d", l=BATCH, c=PASSES, t=TOK)[j]
                return v[:, bass.ds(i, 1), :, :].rearrange("l a t d -> l (a t) d")

            def store(p):
                sp.wait_ge(emptied["W"], p.count(same(EXPERTS), EXPERTS))
                if p.kind == "A":
                    dst = x2[bass.ds(p.i * CHUNK, CHUNK), :].rearrange("(t p) d -> p t d", p=P)
                    sp.dma_start(dst, xo).then_inc(stored, 16)
                    return
                for j in range(4):
                    sp.dma_start(positions(out, p.i, j), xo[32 * j:32 * j + 32, :, :]).then_inc(stored, 16)

            def attention(p, step, n):
                if step == "load" and not (p.kind == "A" and isinstance(p.i, int)):
                    load(p)

            def experts(p, step, n):
                if step == "end":
                    store(p)

            load(Pass("A", 0))
            sp.dma_start(proj_v[:, 0, :], wv).then_inc(rel_landed, 16)
            sp.dma_start(proj_v[:, 1, :], wqkv[2]).then_inc(rel_landed, 16)
            sp.dma_start(proj_o[:, :], wo).then_inc(rel_landed, 16)
            sp.dma_start(raw_b[:, :, :], wqkv[0:2].rearrange("c e i -> e c i")).then_inc(rel_landed, 16)
            sp.wait_ge(setup_dve, 12)
            sp.dma_start(trev_dram, trev).then_inc(trev_stored, 16)
            sp.wait_ge(trev_stored, 16)
            skewed = bass.AP(trev_dram.tensor, trev_dram.offset, [[1, P], [512, HEADS], [1, 3 * P]])
            sp.dma_start(bias_a, skewed).then_inc(bias_landed, 16)
            half = EXPERTS // 2
            for k in range(2 * PIECES):
                if k == 2:
                    sp.wait_ge(flipped, HEADS)
                    sp.wait_ge(setup_dve, 11)
                if k >= PIECES:
                    sp.wait_ge(pieces_cut, k - PIECES + 1)
                e = (k % 2) * half
                if k < 4:
                    src = (wg, wu)[k // 2][:, e:e + half, :]
                    dst = stage[:, k % PIECES, 0:half * INNER].rearrange("p (e c) -> p e c", e=half)
                    sp.dma_start(dst, src).then_inc(piece_landed[k], 16)
                else:
                    src = wd[e:e + half].rearrange("e (t p) h -> p (e t) h", p=P)
                    dst = stage[:, k % PIECES, :].rearrange("p (c h) -> p c h", h=P)
                    sp.dma_start(dst, src).then_inc(piece_landed[k], 16)
            run_passes(sp, attention, experts)
            sp.wait_ge(stored, 16 * (1 + PASSES + 4 * PASSES))

        @block.gpsimd
        def _(pool):
            for s in (kept, hl_ready, h1F_ready, acc_ready):
                pool.sem_inc(s, CREDIT)

            def keep(p):
                pool.wait_ge(x_landed, landed(p))
                pool.wait_ge(normed2, p.count(same(1), 0))
                pool.wait_ge(h1F_ready, p.count(same(1), 0))
                alone(pool)
                if p.kind == "A":
                    pool.tensor_copy(h1[:, :, :], xin[:, :, :]).then_inc(kept, 1)
                else:
                    pool.tensor_tensor(h1[:, :, :], xin[:, :, :], spread(bc[:, 2 * P:3 * P], 1, TOK),
                                       ALU.add).then_inc(kept, 1)

            def attention(p, step, n):
                if step == "norm1":
                    keep(p)

            def experts(p, step, n):
                if step == "begin":
                    if p.kind == "A":
                        pool.wait_ge(h1_part, p.count({"A": 2 * GROUPS, "B": 0}, 2 * GROUPS))
                    else:
                        pool.wait_ge(emptied["S0"], use(p, "S0", last_use(p, "S0")))
                    pool.wait_ge(emptied["W"], p.count(same(EXPERTS), 0))
                    alone(pool)
                    pool.tensor_copy(h1F, h1[:, :, :]).then_inc(h1F_ready, 1)
                elif step == "cut":
                    r = rows_of(n)
                    pool.wait_ge(hh_ready, p.count(same(FT), n + 1))
                    pool.wait_ge(down_done, p.count(same(FT), n + 1 - CUT_RING))
                    pool.tensor_tensor(hid_lo[0:r, n % CUT_RING, :], hid[0:r, n % H_RING, :],
                                       hid_hi[0:r, n % CUT_RING, :].bitcast(F32), ALU.subtract).then_inc(hl_ready, 1)
                elif step == "add" and n > 0:
                    pool.wait_ge(combined, p.count(same(EXPERTS), n + 1))
                    if n > 1:
                        pool.wait_ge(acc_ready, p.count(same(EXPERTS - 1), n - 1))
                    pool.tensor_tensor(acc, acc, part, ALU.add).then_inc(acc_ready, 1)

            first = Pass("A", 0)
            keep(first)
            for k in range(2 * PIECES):
                pool.wait_ge(piece_landed[k], 16)
                if k < 4:
                    width = (EXPERTS // 2) * INNER
                    lo = (k % 2) * width
                    raw = stage[:, k % PIECES, 0:width]
                    hi_dst, lo_dst = w_hi[k // 2][:, lo:lo + width], w_lo[k // 2][:, lo:lo + width]
                else:
                    raw = stage[:, k % PIECES, :]
                    part_of = slice((k % 2) * FT // 2, (k % 2 + 1) * FT // 2)
                    hi_dst = wd_hi[:, part_of, :].rearrange("p c h -> p (c h)")
                    lo_dst = wd_lo[:, part_of, :].rearrange("p c h -> p (c h)")
                    pool.tensor_scalar(raw, raw, 0.5, None, ALU.mult).then_inc(halved, 1)
                    pool.wait_ge(halved, k - 3)
                pool.tensor_copy(hi_dst, raw).then_inc(high_cut, 1)
                pool.wait_ge(high_cut, k + 1)
                pool.tensor_tensor(lo_dst, raw, hi_dst.bitcast(F32), ALU.subtract).then_inc(pieces_cut, 1)
            pool.wait_ge(pieces_cut, 2 * PIECES)

            def attention_but_first(p, step, n):
                if p.kind == "B" or not isinstance(p.i, int):
                    attention(p, step, n)

            run_passes(pool, attention_but_first, experts)

        @block.scalar
        def _(act):
            for h in range(HEADS):
                act.wait_ge(flipped, h + 1)
                act.activation(bias_a[:, h, :], bank["GUYW"[h % 4]][:, 0:3 * P], ACT.Copy).then_inc(bias_ready, 1)
            for s in (exp_done, th_ready, hh_ready, e2_ready):
                act.sem_inc(s, CREDIT)

            def attention(p, step, n):
                if step == "turn1":
                    act.wait_ge(filled["T"], use(p, "T", 0))
                    act.activation(xnT[:, :], bank["T"][:, :], ACT.Copy).then_inc(emptied["T"], 1)
                elif step == "qk":
                    s, g, m = f"S{n % 2}", n // 2, n % 2
                    act.wait_ge(filled[s], use(p, s, g))
                    if p.kind == "A":
                        act.wait_ge(qk_ready, p.count({"A": 2 * GROUPS, "B": 0}, n - 1))
                        dst, b = shifted[:, m, :], bcol[:, m * GROUPS + g:m * GROUPS + g + 1]
                    else:
                        dst, b = (qb, kb)[m][:, g, :], bcol[:, (2 + m) * GROUPS + g:(2 + m) * GROUPS + g + 1]
                    act.activation(dst, bank[s][:, :], ACT.Identity, bias=b).then_inc(emptied[s], 1)
                elif step == "scores":
                    act.wait_ge(emptied[f"S{n % 2}"], use(p, f"S{n % 2}", GROUPS + n // 2))
                    for t in range(2):
                        zt = z[:, n % Z_RING, t * SEQ:(t + 1) * SEQ]
                        last = act.activation(zt, zt, ACT.Exp, bias=nm[:, n % NM_RING, t:t + 1], scale=-1.0)
                    last.then_inc(exp_done, 1)
                elif step == "probs" and n % 4 != 3:
                    turned_out(act, act.copy, p, n)
                elif step == "bscores":
                    s, k = B_BANKS[n]
                    act.wait_ge(emptied[s], use(p, s, k))
                    act.activation(z[:, n, :], z[:, n, :], ACT.Exp).then_inc(exp_done, 1)
                elif step == "bturn":
                    act.wait_ge(filled["T"], use(p, "T", 3))
                    act.activation(ctxT[:, :], bank["T"][:, :], ACT.Copy).then_inc(emptied["T"], 1)
                elif step == "turn2":
                    act.wait_ge(filled["T"], use(p, "T", last_use(p, "T", 3)))
                    act.wait_ge(xl_ready, p.count(same(1), 0))
                    act.activation(xf[:, :], bank["T"][:, :], ACT.Copy).then_inc(emptied["T"], 1)
                elif step == "route":
                    act.wait_ge(gap_ready, p.count(same(1), 1))
                    act.activation(e2[:, :], gap[:, :], ACT.Exp).then_inc(e2_ready, 1)

            def experts(p, step, n):
                if step == "up":
                    r = rows_of(n)
                    act.wait_ge(filled["G"], p.count(same(FT), n + 1))
                    act.wait_ge(h_ready, p.count(same(FT), n - 1))
                    act.activation(th[0:r, n % 2, :], bank["G"][0:r, :], ACT.Tanh, scale=0.5).then_inc(th_ready, 1)
                elif step == "cut":
                    r = rows_of(n)
                    act.wait_ge(h_ready, p.count(same(FT), n + 1))
                    act.wait_ge(down_done, p.count(same(FT), n + 1 - CUT_RING))
                    act.activation(hid_hi[0:r, n % CUT_RING, :], hid[0:r, n % H_RING, :], ACT.Copy
                                   ).then_inc(hh_ready, 1)
                elif step == "weight":
                    act.wait_ge(filled["W"], p.count(same(EXPERTS), n))
                    act.wait_ge(combined, p.count(same(EXPERTS), n))
                    act.activation(wbS, bank["W"][:, :], ACT.Copy).then_inc(emptied["W"], 1)

            passes = [attention, experts]

            def experts_after_cuts(p, step, n):
                if step == "begin" and p.kind == "A":
                    act.wait_ge(pieces_cut, 2 * PIECES)
                passes[1](p, step, n)

            act.wait_ge(setup_dve, 14)
            run_passes(act, attention, experts_after_cuts)

        @block.vector
        def _(dve):
            for s in (emptied["S0"], emptied["S1"], emptied["T"], emptied["O"], emptied["W"], normed1, qk_ready,
                      turned, h1_part, normed2, gap_ready, wcat_ready, xh_ready, xl_ready, wTF_ready,
                      a_ready, h_ready, combined):
                dve.sem_inc(s, CREDIT)
            dve.memset(ones[:, :], 1.0).then_inc(setup_dve, 1)
            dve.memset(row_bc[:, 3 * P:3 * P + 8], -FAR).then_inc(setup_dve, 1)
            dve.memset(router[:, :], 0.0).then_inc(setup_dve, 1)
            dve.memset(vx[:, :, :], 1.0).then_inc(setup_dve, 1)
            dve.wait_ge(w_landed, 7 * 16)
            dve.tensor_scalar(head_cols(proj[:, 0, :], 4), spread(raw_a[:, 0, :].rearrange("p (h d) -> p h d", h=HEADS), 2, 4),
                              SCALE, None, ALU.mult).then_inc(setup_dve, 1)
            dve.tensor_copy(head_cols(proj[:, 1, :], 4), spread(raw_a[:, 1, :].rearrange("p (h d) -> p h d", h=HEADS), 2, 4)
                            ).then_inc(setup_dve, 1)
            dve.wait_ge(row_landed, 8 * 16)
            for m in range(4):
                src = spread(row_raw[:, m, :].rearrange("p (h d) -> p h d", h=HEADS), 2, 4)
                dve.tensor_scalar(head_cols(row_rep[:, m, :], 4), src, SCALE if m % 2 == 0 else 1.0, None,
                                  ALU.mult).then_inc(setup_dve, 1)
            dve.tensor_copy(sel[:, :], sel_raw).then_inc(setup_dve, 1)
            dve.wait_ge(setup_pe, 1)
            dve.tensor_copy(trev, bank["O"][0:HEADS, :]).then_inc(setup_dve, 1)
            dve.wait_ge(setup_pe, 2)
            dve.tensor_copy(bcol[:, :], bank["S0"][:, 0:4 * GROUPS]).then_inc(setup_dve, 1)
            dve.wait_ge(setup_pe, 3)
            dve.tensor_copy(bc[:, :], bank["T"][:, 0:3 * P + 8]).then_inc(setup_dve, 1)

            steps = [0]

            def then(p, instruction):
                steps[0] += 1
                instruction.then_inc(vstep, 1)
                dve.wait_ge(vstep, steps[0])


            def normalise(p, rows, done):
                for t in range(TOK):
                    last = dve.bn_stats(stats[:, t, :], rows[:, t, :])
                then(p, last)
                for t in range(TOK):
                    last = dve.bn_aggr(moments[:, t, :], stats[:, t, :])
                then(p, last)
                v, y, a, b = (rs[:, k, :] for k in range(4))
                then(p, dve.tensor_scalar(v, moments[:, :, 1], EPS, None, ALU.add))
                then(p, dve.tensor_scalar(y.bitcast(I32), v.bitcast(I32), -0.5, MAGIC, ALU.mult, ALU.add))
                for _ in range(NEWTON):
                    then(p, dve.scalar_tensor_tensor(out=a, in0=y, scalar=-0.5, in1=y, op0=ALU.mult, op1=ALU.mult))
                    then(p, dve.tensor_tensor(b, a, v, ALU.mult))
                    then(p, dve.scalar_tensor_tensor(out=y, in0=b, scalar=1.5, in1=y, op0=ALU.add, op1=ALU.mult))
                for t in range(TOK):
                    last = dve.tensor_scalar(xn[:, t, :], rows[:, t, :], moments[:, t, 0:1], y[:, t:t + 1],
                                             ALU.subtract, ALU.mult)
                last.then_inc(done, 1)

            def route(p):
                for t in range(TOK):
                    last = dve.max(top[:, t, :], lg[:, t, :])
                then(p, last)
                for t in range(TOK):
                    last = dve.max_index(at[:, t, :], top[:, t, :], lg[:, t, :])
                then(p, last)
                dve.tensor_tensor(gap[:, :], top[:, :, 1], top[:, :, 0], ALU.subtract).then_inc(gap_ready, 1)
                then(p, dve.tensor_copy(atf[:, :, :], at[:, :, :]))
                s, first, second = (share[:, k, :] for k in range(3))
                dve.wait_ge(e2_ready, p.count(same(1), 1))
                then(p, dve.tensor_scalar(s, e2[:, :], 1.0, None, ALU.add))
                then(p, dve.reciprocal(first, s))
                then(p, dve.tensor_tensor(second, e2[:, :], first, ALU.mult))
                for t in range(TOK):
                    for k, w in enumerate((first, second)):
                        last = dve.tensor_scalar(wtok[:, k, t, :], cst[:, C_IOTA:C_IOTA + 8], atf[:, t, k:k + 1],
                                                 w[:, t:t + 1], ALU.is_equal, ALU.mult)
                then(p, last)
                then(p, dve.tensor_tensor(wtok[:, 2, :, :], wtok[:, 0, :, :], wtok[:, 1, :, :], ALU.add))
                then(p, dve.tensor_copy(whi[:, :, :], wtok[:, 2, :, :]))
                dve.tensor_copy(wcat[:, :, 0:8], whi[:, :, :].bitcast(F32))
                dve.tensor_tensor(wcat[:, :, 8:16], wtok[:, 2, :, :], whi[:, :, :].bitcast(F32),
                                  ALU.subtract).then_inc(wcat_ready, 1)

            def attention(p, step, n):
                if step == "norm1":
                    steps[0] = 1
                    dve.sem_clear(vstep)
                    dve.sem_inc(vstep, 1)
                    dve.wait_ge(x_landed, landed(p))
                    normalise(p, xin, normed1)
                elif step == "qk" and p.kind == "A":
                    s, g, m = f"S{n % 2}", n // 2, n % 2
                    dve.wait_ge(emptied[s], use(p, s, g))
                    dve.wait_ge(qk_ready, p.count({"A": 2 * GROUPS, "B": 0}, n))
                    then(p, dve.tensor_copy(high[:, :], shifted[:, m, :]))
                    mask = cst[:, C_MQ + m:C_MQ + m + 1]
                    dve.scalar_tensor_tensor(out=(qx, kx)[m][:, g, :], in0=high[:, :].bitcast(F32), scalar=mask,
                                             in1=shifted[:, m, :], op0=ALU.mult, op1=ALU.add).then_inc(qk_ready, 1)
                elif step == "v":
                    m = "AB".index(p.kind)
                    dve.wait_ge(filled["T"], use(p, "T", 1))
                    dst = vx[:, :, 0:HEADS * VW].rearrange("p t (h c) -> p t h c", c=VW)[:, :, :, 0:DH]
                    src = bank["T"][:, :].rearrange("p (t h d) -> p t h d", t=TOK, d=DH)
                    b = spread(bc[:, m * P:(m + 1) * P].rearrange("p (h d) -> p h d", d=DH), 1, TOK)
                    dve.tensor_tensor(dst, src, b, ALU.add).then_inc(emptied["T"], 1)
                elif step == "scores":
                    s, h = f"S{n % 2}", n % HEADS
                    if n == 0:
                        dve.wait_ge(bias_ready, HEADS)
                    dve.wait_ge(filled[s], use(p, s, GROUPS + n // 2))
                    dve.wait_ge(filled["T"], use(p, "T", 2 + n - Z_RING))
                    alone(dve)
                    for t in range(2):
                        last = dve.tensor_tensor_reduce(
                            z[:, n % Z_RING, t * SEQ:(t + 1) * SEQ], bank[s][:, t * SEQ:(t + 1) * SEQ],
                            bias_a[:, h, P - P * t:P - P * t + SEQ], -1.0, FAR, ALU.add, ALU.min,
                            nm[:, n % NM_RING, t:t + 1])
                    last.then_inc(emptied[s], 1)
                elif step == "probs" and n % 4 == 3:
                    turned_out(dve, dve.tensor_copy, p, n)
                elif step == "mix":
                    dve.wait_ge(filled["O"], use(p, "O", 2 * n))
                    dve.tensor_copy(oT[:, n % 2, :], bank["O"][:, 0:SEQ]).then_inc(emptied["O"], 1)
                elif step == "context":
                    dve.wait_ge(filled["O"], use(p, "O", 2 * n + 1))
                    o = bank["O"][:, 0:SEQ].rearrange("p (t j c) -> p (t j) c", t=2, j=4)
                    c8 = ctxt[:, :, :, :].rearrange("p t j d -> p (t j) d")
                    then(p, dve.reciprocal(rec[:, 0:8], o[:, :, DH]))
                    dve.tensor_tensor(c8, o[:, :, 0:DH], spread(rec[:, 0:8], 2, DH), ALU.mult).then_inc(emptied["O"], 1)
                    dve.wait_ge(emptied["O"], use(p, "O", 2 * n + 1))
                    dve.wait_ge(kept, p.count(same(1), 1))
                    b, g = n // GROUPS, n % GROUPS
                    dst = h1[:, 2 * b:2 * b + 2, 32 * g:32 * g + 32]
                    dve.tensor_tensor(dst, dst, ctxt[:, :, :, :].rearrange("p t j d -> p t (j d)"), ALU.add
                                      ).then_inc(h1_part, 1)
                elif step == "bscores":
                    s, k = B_BANKS[n]
                    dve.wait_ge(filled[s], use(p, s, k))
                    sc = bank[s][:, :].rearrange("p (h m) -> p h m", m=32)
                    then(p, dve.tensor_reduce(maxb[:, n, :], sc, AX.X, ALU.max))
                    dve.wait_ge(turned, p.count({"A": 0, "B": 4}, n - 3))
                    dve.tensor_tensor(z[:, n, :].rearrange("p (h m) -> p h m", m=32), sc,
                                      spread(maxb[:, n, :], 2, 32), ALU.subtract).then_inc(emptied[s], 1)
                elif step == "bprobs":
                    dve.wait_ge(exp_done, p.count(PASS_SCORES, n + 1))
                    dve.transpose(probT[:, n, :], z[:, n, :]).then_inc(turned, 1)
                elif step == "bmix":
                    dve.wait_ge(filled["O"], use(p, "O", 1 + n))
                    o = bank["O"][:, 0:HEADS * VW].rearrange("p (h c) -> p h c", c=VW)
                    then(p, dve.reciprocal(rec[:, :], o[:, :, DH]))
                    dve.tensor_tensor(ctxb[:, n, :].rearrange("p (h d) -> p h d", d=DH), o[:, :, 0:DH],
                                      spread(rec[:, :], 2, DH), ALU.mult).then_inc(emptied["O"], 1)
                elif step == "bout":
                    dve.wait_ge(filled["S0"], use(p, "S0", last_use(p, "S0")))
                    dve.wait_ge(kept, p.count(same(1), 1))
                    o = bank["S0"][:, :].rearrange("p (t d) -> p t d", t=TOK)
                    dve.tensor_tensor(h1[:, :, :], h1[:, :, :], o, ALU.add).then_inc(emptied["S0"], 1)
                elif step == "norm2":
                    if p.kind == "A":
                        dve.wait_ge(h1_part, p.count({"A": 2 * GROUPS, "B": 0}, 2 * GROUPS))
                    else:
                        dve.wait_ge(emptied["S0"], use(p, "S0", last_use(p, "S0")))
                    normalise(p, h1, normed2)
                elif step == "logits":
                    dve.wait_ge(filled["T"], use(p, "T", last_use(p, "T", 2)))
                    dve.tensor_tensor(lg[:, :, :], bank["T"][:, 0:8 * TOK].rearrange("p (t e) -> p t e", t=TOK),
                                      spread(bc[:, 3 * P:3 * P + 8], 1, TOK), ALU.add).then_inc(emptied["T"], 1)
                    dve.wait_ge(emptied["T"], use(p, "T", last_use(p, "T", 2)))
                    alone(dve)
                elif step == "route":
                    route(p)
                elif step == "wturn":
                    dve.wait_ge(filled["T"], use(p, "T", last_use(p, "T")))
                    dve.tensor_copy(wts[:, :], bank["T"][0:16, :]).then_inc(emptied["T"], 1)

            def experts(p, step, n):
                if step == "begin":
                    if p.kind == "A":
                        dve.wait_ge(pieces_cut, 2 * PIECES)
                    dve.wait_ge(filled["W"], p.count(same(EXPERTS), 0))
                    dve.wait_ge(emptied["T"], use(p, "T", last_use(p, "T")))
                    dve.tensor_copy(xh[:, :], xf[:, :]).then_inc(xh_ready, 1)
                    dve.wait_ge(xh_ready, p.count(same(1), 1))
                    dve.tensor_tensor(xl[:, :], xf[:, :], xh[:, :].bitcast(F32), ALU.subtract).then_inc(xl_ready, 1)
                    dve.tensor_copy(wTF[:, :], wts[:, :]).then_inc(wTF_ready, 1)
                elif step == "up":
                    r = rows_of(n)
                    dve.wait_ge(th_ready, p.count(same(FT), n + 1))
                    a = th[0:r, n % 2, :]
                    dve.scalar_tensor_tensor(out=a, in0=a, scalar=1.0, in1=bank["G"][0:r, :], op0=ALU.add,
                                             op1=ALU.mult).then_inc(a_ready, 1)
                elif step == "gate":
                    r = rows_of(n)
                    dve.wait_ge(a_ready, p.count(same(FT), n + 1))
                    dve.wait_ge(filled["U"], p.count(same(FT), n + 1))
                    dve.wait_ge(hl_ready, p.count(same(FT), n + 1 - H_RING))
                    dve.tensor_tensor(hid[0:r, n % H_RING, :], th[0:r, n % 2, :], bank["U"][0:r, :], ALU.mult
                                      ).then_inc(h_ready, 1)
                elif step == "add":
                    dve.wait_ge(down_done, p.count(same(FT), TILES_I * (n + 1)))
                    if n == 0:
                        dve.wait_ge(filled["W"], p.count(same(EXPERTS), 0))
                        dve.tensor_copy(acc, bank["Y"][:, :]).then_inc(combined, 1)
                    else:
                        dve.wait_ge(emptied["W"], p.count(same(EXPERTS), n))
                        dve.wait_ge(acc_ready, p.count(same(EXPERTS - 1), n - 1))
                        dve.tensor_tensor(part, bank["Y"][:, :], wbS, ALU.mult).then_inc(combined, 1)
                elif step == "end":
                    dve.wait_ge(filled["W"], p.count(same(EXPERTS), EXPERTS))
                    dve.wait_ge(h1F_ready, p.count(same(1), 1))
                    dve.wait_ge(stored, p.i * 16 + 16 if p.kind == "A" else p.i * 64 + 16 * (PASSES + 1))
                    dve.tensor_tensor(xo, bank["W"][:, :].rearrange("p (t d) -> p t d", t=TOK), h1F, ALU.add
                                      ).then_inc(emptied["W"], 1)

            def with_weights(p, step, n):
                if p.kind == "B" and isinstance(p.i, int) and step == "load":
                    dve.wait_ge(rel_landed, 4 * 16)
                    for m in range(2):
                        src = spread(raw_b[:, m, :].rearrange("p (h d) -> p h d", h=HEADS), 2, 4)
                        dve.tensor_scalar(head_cols(proj[:, m, :], 4), src, 1.0 if m else SCALE, None, ALU.mult
                                          ).then_inc(proj_b_ready, 1)
                attention(p, step, n)

            run_passes(dve, with_weights, experts)

        @block.tensor
        def _(pe):
            for s in list(filled.values()) + [down_done]:
                pe.sem_inc(s, CREDIT)
            pe.wait_ge(w_landed, 7 * 16)
            pe.matmul(bank["O"][0:HEADS, :], relb, hot, start=True, stop=True).then_inc(setup_pe, 1)
            pe.wait_ge(setup_dve, 10)
            for m in range(4):
                for g in range(GROUPS):
                    c = m * GROUPS + g
                    last = pe.matmul(bank["S0"][:, c:c + 1], row_rep[:, m, g * P:(g + 1) * P], ones[:, 0:1],
                                     start=True, stop=True)
            last.then_inc(setup_pe, 1)
            pe.matmul(bank["T"][:, 0:3 * P + 8], ones[:, :], row_bc, start=True, stop=True).then_inc(setup_pe, 1)
            pe.wait_ge(bias_landed, 16)
            for h in range(HEADS):
                if h >= 4:
                    pe.wait_ge(bias_ready, h - 3)
                pe.matmul(bank["GUYW"[h % 4]][:, 0:3 * P], flip, bias_a[:, h, :], start=True, stop=True
                          ).then_inc(flipped, 1)
            pe.wait_ge(setup_dve, 14)
            pe.wait_ge(rel_landed, 4 * 16)

            def next_use(p, name, n):
                pe.wait_ge(emptied[name], use(p, name, n - 1))

            def turn_rows(p, rows, n):
                next_use(p, "T", n)
                for t in range(TOK):
                    last = pe.transpose(bank["T"][:, t * P:(t + 1) * P], rows[:, t, :], ident)
                last.then_inc(filled["T"], 1)

            def attention(p, step, n):
                half = "AB".index(p.kind)
                if step == "turn1":
                    pe.wait_ge(normed1, p.count(same(1), 1))
                    turn_rows(p, xn, 0)
                elif step == "qk":
                    s, g, m = f"S{n % 2}", n // 2, n % 2
                    pe.wait_ge(emptied["T"], use(p, "T", 0))
                    if half and isinstance(p.i, int):
                        pe.wait_ge(proj_b_ready, 2)
                    next_use(p, s, g)
                    pe.matmul(bank[s][:, :], proj[:, m, g * P:(g + 1) * P], xnT[:, :], start=True, stop=True
                              ).then_inc(filled[s], 1)
                elif step == "v":
                    next_use(p, "T", 1)
                    for t in range(TOK):
                        last = pe.matmul(bank["T"][:, t * P:(t + 1) * P], xnT[:, t * P:(t + 1) * P],
                                         proj_v[:, half, :], start=True, stop=True)
                    last.then_inc(filled["T"], 1)
                elif step == "scores":
                    s, b, h = f"S{n % 2}", n // HEADS, n % HEADS
                    rows, g = slice(32 * (h % 4), 32 * (h % 4) + 32), h // 4
                    pe.wait_ge(qk_ready, p.count({"A": 2 * GROUPS, "B": 0}, 2 * GROUPS))
                    next_use(p, s, GROUPS + n // 2)
                    for t in range(2):
                        lo = b * SEQ + t * P
                        last = pe.matmul(bank[s][:, t * SEQ:(t + 1) * SEQ], qx[rows, g, lo:lo + P],
                                         kx[rows, g, b * SEQ:(b + 1) * SEQ], start=True, stop=True)
                    last.then_inc(filled[s], 1)
                elif step == "probs":
                    pe.wait_ge(exp_done, p.count(PASS_SCORES, n + 1))
                    next_use(p, "T", 2 + n)
                    for k in range(2):
                        for t in range(2):
                            c = k * SEQ + t * P
                            last = pe.transpose(bank["T"][:, c:c + P],
                                                z[:, n % Z_RING, t * SEQ + k * P:t * SEQ + (k + 1) * P], ident)
                    last.then_inc(filled["T"], 1)
                elif step == "mix":
                    pe.wait_ge(emptied["T"], use(p, "T", 2 + 4 * n + 3))
                    next_use(p, "O", 2 * n)
                    b, g = n // GROUPS, n % GROUPS
                    for k in range(2):
                        for j in range(4):
                            u, c = 4 * n + j, (4 * g + j) * VW
                            last = pe.matmul(bank["O"][32 * j:32 * j + 32, 0:SEQ], vx[:, 2 * b + k, c:c + 32],
                                             probT[:, u % PT_RING, k * SEQ:(k + 1) * SEQ], start=(k == 0),
                                             stop=(k == 1), tile_position=(0, 32 * j))
                    last.then_inc(filled["O"], 1)
                elif step == "context":
                    next_use(p, "O", 2 * n + 1)
                    for t in range(2):
                        last = pe.transpose(bank["O"][:, t * P:(t + 1) * P], oT[:, n % 2, t * P:(t + 1) * P], ident)
                    last.then_inc(filled["O"], 1)
                elif step == "bscores":
                    s, use_s = B_BANKS[n]
                    for k in range(2):
                        pe.wait_ge(emptied[f"S{k}"], use(p, f"S{k}", GROUPS - 1))
                    next_use(p, s, use_s)
                    alone(pe)
                    rows = slice(32 * n, 32 * n + DH)
                    for t in range(TOK):
                        for g in range(GROUPS):
                            c = (t * GROUPS + g) * 32
                            for j in range(4):
                                lo = t * P + 32 * j
                                last = pe.matmul(bank[s][32 * j:32 * j + 32, c:c + 32], qb[rows, g, lo:lo + 32],
                                                 kb[rows, g, lo:lo + 32], start=True, stop=True,
                                                 tile_position=(32 * n, 32 * j))
                    last.then_inc(filled[s], 1)
                elif step == "bmix":
                    pe.wait_ge(turned, p.count({"A": 0, "B": 4}, 4))
                    next_use(p, "O", 1 + n)
                    alone(pe)
                    for h in range(HEADS):
                        c = (n * GROUPS + h // 4) * 32
                        for j in range(4):
                            r = slice(32 * j, 32 * j + 32)
                            last = pe.matmul(bank["O"][r, h * VW:(h + 1) * VW], probT[r, h % 4, c:c + 32],
                                             vx[r, n, h * VW:(h + 1) * VW], start=True, stop=True,
                                             tile_position=(32 * j, 32 * j))
                    last.then_inc(filled["O"], 1)
                elif step == "bturn":
                    pe.wait_ge(emptied["O"], use(p, "O", TOK))
                    turn_rows(p, ctxb, 3)
                elif step == "bout":
                    pe.wait_ge(emptied["T"], use(p, "T", 3))
                    next_use(p, "S0", last_use(p, "S0"))
                    for t in range(TOK):
                        last = pe.matmul(bank["S0"][:, t * P:(t + 1) * P], ctxT[:, t * P:(t + 1) * P], proj_o[:, :],
                                         start=True, stop=True)
                    last.then_inc(filled["S0"], 1)
                elif step == "turn2":
                    pe.wait_ge(normed2, p.count(same(1), 1))
                    turn_rows(p, xn, last_use(p, "T", 3))
                elif step == "logits":
                    next_use(p, "T", last_use(p, "T", 2))
                    for t in range(TOK):
                        last = pe.matmul(bank["T"][:, 8 * t:8 * t + 8], xf[:, t * P:(t + 1) * P], router[:, :],
                                         start=True, stop=True)
                    last.then_inc(filled["T"], 1)
                elif step == "wturn":
                    pe.wait_ge(wcat_ready, p.count(same(1), 1))
                    next_use(p, "T", last_use(p, "T"))
                    for t in range(TOK):
                        last = pe.transpose(bank["T"][0:16, t * P:(t + 1) * P], wcat[:, t, :], ident)
                    last.then_inc(filled["T"], 1)

            def product(dst, high_w, low_w, high_x, low_x, start=True, stop=True):
                pe.matmul(dst, high_w, high_x, start=start, stop=False)
                pe.matmul(dst, high_w, low_x, start=False, stop=False)
                return pe.matmul(dst, low_w, high_x, start=False, stop=stop)

            def experts(p, step, n):
                if step == "begin":
                    pe.wait_ge(wTF_ready, p.count(same(1), 1))
                    if p.kind == "A":
                        pe.wait_ge(pieces_cut, 2 * PIECES)
                elif step == "up":
                    r, c = rows_of(n), cols_of(n)
                    pe.wait_ge(a_ready, p.count(same(FT), n))
                    product(bank["G"][0:r, :], w_hi[0][:, c], w_lo[0][:, c], xh[:, :], xl[:, :]
                            ).then_inc(filled["G"], 1)
                    pe.wait_ge(h_ready, p.count(same(FT), n))
                    product(bank["U"][0:r, :], w_hi[1][:, c], w_lo[1][:, c], xh[:, :], xl[:, :]
                            ).then_inc(filled["U"], 1)
                elif step == "down":
                    r, e, k = rows_of(n), n // TILES_I, n % TILES_I
                    pe.wait_ge(hl_ready, p.count(same(FT), n + 1))
                    if k == 0:
                        pe.wait_ge(combined, p.count(same(EXPERTS), e))
                    ins = product(bank["Y"][:, :], wd_hi[0:r, n, :], wd_lo[0:r, n, :], hid_hi[0:r, n % CUT_RING, :],
                                  hid_lo[0:r, n % CUT_RING, :], start=(k == 0), stop=(k == TILES_I - 1))
                    ins.then_inc(down_done, 1)
                elif step == "weight":
                    pe.wait_ge(emptied["W"], p.count(same(EXPERTS), n - 1))
                    pe.matmul(bank["W"][:, :], sel[:, (n - 1) * P:n * P], wTF[:, :], start=True, stop=True
                              ).then_inc(filled["W"], 1)
                elif step == "end":
                    pe.wait_ge(acc_ready, p.count(same(EXPERTS - 1), EXPERTS - 1))
                    pe.wait_ge(emptied["W"], p.count(same(EXPERTS), EXPERTS - 1))
                    for t in range(TOK):
                        last = pe.transpose(bank["W"][:, t * P:(t + 1) * P], acc[:, t * P:(t + 1) * P], ident)
                    last.then_inc(filled["W"], 1)

            run_passes(pe, attention, experts)


def kernel(**inputs):
    import concourse.bacc as bacc
    from concourse.bass_utils import run_bass_kernel_spmd

    def a(name):
        return np.asarray(inputs["L0_" + name])

    row = lambda t: t.reshape(1, -1)
    inner_first = lambda shared, routed: np.concatenate([shared[None], routed]).transpose(2, 0, 1)
    down = np.concatenate([a("ffn_sd")[None], a("ffn_rd")]).transpose(0, 2, 1)
    arrays = {
        "x": a("attn_a_hidden_states").reshape(BATCH * SEQ, D),
        "wq": a("attn_a_Wq"), "bq": row(a("attn_a_bq")), "wk": a("attn_a_Wk"), "bk": row(a("attn_a_bk")),
        "wv": a("attn_a_Wv"), "bv": row(a("attn_a_bv")), "rel": a("attn_a_rel_bias"),
        "wqkv": a("attn_b_qkv_proj").reshape(P, 3, D).transpose(1, 2, 0),
        "bqkv": a("attn_b_qkv_bias").reshape(P, 3).T.reshape(1, 3, P),
        "wo": a("attn_b_out_proj").T, "bo": row(a("attn_b_out_bias")),
        "wg": inner_first(a("ffn_sg"), a("ffn_rg")), "wu": inner_first(a("ffn_su"), a("ffn_ru")),
        "wd": np.concatenate([down, np.zeros((EXPERTS, P * TILES_I - INNER, D), down.dtype)], axis=1),
        "wr": a("ffn_wr").T, "rb": row(a("ffn_rb")), "const": constants(),
    }
    arrays = {f"in_{k}": np.ascontiguousarray(v) for k, v in arrays.items()}
    nc = bacc.Bacc("TRN2", target_bir_lowering=False, num_devices=1)
    args = [nc.dram_tensor(k, v.shape, mybir.dt.from_np(v.dtype), kind="ExternalInput").ap() for k, v in arrays.items()]
    out = nc.dram_tensor("out_x", (BATCH * SEQ, D), F32, kind="ExternalOutput").ap()
    program(nc, *args, out)
    result = run_bass_kernel_spmd(nc, [arrays], core_ids=[0])
    return result.results[0]["out_x"].reshape(BATCH, SEQ, D)
```

```python
import numpy as np
import concourse.bass as bass
from concourse import mybir

F32 = mybir.dt.float32
F32R = mybir.dt.float32r
I32 = mybir.dt.int32
U32 = mybir.dt.uint32
ALU = mybir.AluOpType
ACT = mybir.ActivationFunctionType
AX = mybir.AxisListType

P = 128
BATCH, SEQ, D = 32, 256, 128
HEADS, DH = 16, 8
BUCKETS = 32
EXPERTS, INNER = 8, 352
TILES_I = 3
CHUNK = 512
TOK = CHUNK // P
PASSES = BATCH * SEQ // CHUNK
POS = CHUNK // BATCH
GROUPS = HEADS // 4
UNITS = 2 * HEADS
FT = EXPERTS * TILES_I
EPS = 1e-5
MAGIC = float(0x5F3759DF)
NEWTON = 3
FAR = 3.0e38

CREDIT = 8

Z_RING = 4
PT_RING = 5
NM_RING = 8
H_RING = 2
CUT_RING = 3
DOWN_LAG = 1
COPIES = 8

VW = DH + 1
STAGE, PIECES = 1536, 3
SCALE = float(DH) ** -0.5

USES = {"A": {"S0": 20, "S1": 20, "T": 5 + UNITS, "O": 2 * 2 * GROUPS},
        "B": {"S0": 6, "S1": 5, "T": 7, "O": 1 + TOK}}

C_ID, C_MQ, C_MK, C_IOTA, C_HOT = 0, 128, 129, 130, 138
C_FLIP = C_HOT + 512
C_KEPT = C_HOT
C_ALL = C_FLIP + P


def constants():
    c = np.zeros((P, C_ALL), np.float32)
    c[:, C_ID:C_ID + P] = np.eye(P)
    row = np.arange(P) % 32 // 8
    c[:, C_MQ] = np.where(row >= 2, -1.0, 0.0)
    c[:, C_MK] = np.where(row % 2 == 1, -1.0, 0.0)
    c[:, C_IOTA:C_IOTA + 8] = np.arange(8)
    exact = BUCKETS // 2
    for x in range(2 * SEQ - 1):
        n = max(SEQ - 1 - x, 0)
        if n < exact:
            b = n
        else:
            ratio = np.log(np.float32(n) / np.float32(exact)) / np.float32(np.log(BUCKETS / exact))
            b = min(exact + int(ratio * np.float32(BUCKETS - exact)), BUCKETS - 1)
        c[b, C_HOT + x] = 1.0
    c[:, C_FLIP:C_FLIP + P] = np.eye(P)[::-1]
    return c


class Pass:

    def __init__(self, kind, i):
        self.kind, self.i = kind, i
        self.g = i if kind == "A" else i + PASSES

    def count(self, per, n):
        before = 0 if self.kind == "A" else PASSES * per["A"]
        return self.i * per[self.kind] + (CREDIT + before + n)


def same(n):
    return {"A": n, "B": n}


NORM_PARTS, ROUTE_PARTS = 4 + NEWTON, 5

WORK = {
    "norm1": {"dve": 0.6, "pool": 1.8}, "turn1": {"pe": 0.5, "act": 0.5}, "qk": {"pe": 0.85, "act": 0.6, "dve": 1.1},
    "v": {"pe": 0.9, "dve": 0.6}, "scores": {"pe": 0.25, "dve": 0.75, "act": 0.8}, "probs": {"pe": 0.45, "act": 0.5},
    "mix": {"pe": 1.0, "dve": 0.35}, "context": {"pe": 0.25, "dve": 0.7}, "norm2": {"dve": 0.6},
    "turn2": {"pe": 0.5, "act": 0.5}, "logits": {"pe": 1.6, "dve": 0.3}, "route": {"dve": 0.6, "act": 0.1},
    "wturn": {"pe": 0.5, "dve": 0.6}, "bscores": {"pe": 0.5, "dve": 1.4, "act": 0.5}, "bprobs": {"dve": 0.6},
    "bmix": {"pe": 0.35, "dve": 0.6}, "bturn": {"pe": 0.5, "act": 0.5}, "bout": {"pe": 0.9, "dve": 0.6},
    "begin": {"dve": 1.0, "pe": 0.1, "pool": 1.8}, "gate": {"pe": 0.65, "act": 0.5, "dve": 0.6},
    "up": {"pe": 0.65, "dve": 0.6}, "cut": {"act": 0.55, "pool": 1.25}, "down": {"pe": 0.65},
    "add": {"dve": 0.6, "pool": 1.25}, "end": {"pe": 0.5, "dve": 0.6, "act": 0.1},
}
HAND_OVER, OWN = 0.15, 0.06
FLOW = ("pe", "act", "dve", "pool")


def needs_attention(kind, eng, step, n):
    if step == "norm1":
        return [("pool", "begin", 0)] if eng == "pool" else [("dve", "norm1", n - 1)] if n else []
    if step == "turn1":
        return [("dve", "norm1", NORM_PARTS - 1)] if eng == "pe" else [("pe", "turn1", 0)]
    if step == "qk":
        last = "dve" if kind == "A" else "act"
        if eng == "pe":
            return [("act", "turn1", 0)] + ([("act", "qk", n - 2)] if n > 1 else [])
        if eng == "act":
            return [("pe", "qk", n)] + ([(last, "qk", n - 2)] if n > 1 else [])
        return [("act", "qk", n)]
    if step == "v":
        return [("act", "turn1", 0)] if eng == "pe" else [("pe", "v", 0)]
    if step == "scores":
        if eng == "pe":
            return [("dve", "qk", 2 * GROUPS - 1)] + ([("dve", "scores", n - 2)] if n > 1 else [])
        if eng == "dve":
            return [("pe", "scores", n)] + ([("pe", "probs", n - Z_RING)] if n >= Z_RING else [])
        return [("dve", "scores", n)]
    if step == "probs":
        if eng == "pe":
            return [("act", "scores", n), ("act", "probs", n - 1) if n else ("dve", "v", 0)]
        return [("pe", "probs", n)] + ([("pe", "mix", (n - PT_RING) // 4)] if n >= PT_RING else [])
    if step == "mix":
        if eng == "pe":
            return [("act", "probs", 4 * n + 3)] + ([("dve", "context", n - 1)] if n else [])
        return [("pe", "mix", n)]
    if step == "context":
        return [("dve", "mix", n)] if eng == "pe" else [("pe", "context", n), ("pool", "norm1", 0)]
    if step == "bscores":
        if eng == "pe":
            return [("act", "qk", 2 * GROUPS - 1), ("act", "qk", 2 * GROUPS - 2), ("dve", "v", 0)]
        return [("pe", "bscores", n)] if eng == "dve" else [("dve", "bscores", n)]
    if step == "bprobs":
        return [("act", "bscores", 4 * n + 3)]
    if step == "bmix":
        if eng == "pe":
            return [("dve", "bprobs", 3)] + ([("dve", "bmix", n // 4 * 4 - 1)] if n > 3 else [])
        return [("pe", "bmix", n)]
    if step == "bturn":
        return [("dve", "bmix", 4 * TOK - 1)] if eng == "pe" else [("pe", "bturn", 0)]
    if step == "bout":
        return [("act", "bturn", 0)] if eng == "pe" else [("pe", "bout", 0), ("pool", "norm1", 0)]
    if step == "norm2":
        return [("dve", "norm2", n - 1) if n else ("dve", "context", 2 * GROUPS - 1) if kind == "A"
                else ("dve", "bout", 0)]
    if step == "turn2":
        return [("dve", "norm2", NORM_PARTS - 1)] if eng == "pe" else [("pe", "turn2", 0), ("dve", "begin", 0)]
    if step == "logits":
        return [("act", "turn2", 0)] if eng == "pe" else [("pe", "logits", 0)]
    if step == "route":
        if eng == "act":
            return [("dve", "route", 1)]
        return [("dve", "route", n - 1) if n else ("dve", "logits", 0)] + ([("act", "route", 1)] if n == 3 else [])
    if step == "wturn":
        return [("dve", "route", ROUTE_PARTS - 1), ("dve", "begin", 0)] if eng == "pe" else [("pe", "wturn", 0)]


def needs_experts(eng, step, n):
    if step == "begin":
        return [("dve", "begin", 0)] if eng == "pe" else []
    if step == "gate":
        if eng == "pe":
            return [("dve", "up", n - 2)] if n > 1 else [("pe", "begin", 0)]
        if eng == "act":
            return [("pe", "gate", n)] + ([("dve", "up", n - 2)] if n > 1 else [])
        return [("act", "gate", n)]
    if step == "up":
        if eng == "pe":
            return [("dve", "gate", n - 1)] if n else [("pe", "begin", 0)]
        return [("pe", "up", n), ("dve", "gate", n)] + ([("pool", "cut", n - H_RING)] if n >= H_RING else [])
    if step == "cut":
        if eng == "act":
            return [("dve", "up", n)] + ([("pe", "down", n - CUT_RING)] if n >= CUT_RING else [])
        return [("act", "cut", n)]
    if step == "down":
        e = n // TILES_I
        return [("pool", "cut", n)] + ([("dve", "add", e - 1)] if n % TILES_I == 0 and e else [])
    if step == "add":
        if eng == "dve":
            return [("pe", "down", TILES_I * n + TILES_I - 1)] + ([("pool", "add", n - 1)] if n > 1 else [])
        return [("dve", "add", n)]
    if step == "end":
        if eng == "pe":
            return [("pool", "add", EXPERTS - 1)]
        return [("pe", "end", 0)] if eng == "dve" else [("dve", "end", 0)]


def steps_attention(kind):
    out = [("norm1", n) for n in range(NORM_PARTS)] + [("turn1", 0)]
    out += [("qk", n) for n in range(2 * GROUPS)] + [("v", 0)]
    if kind == "A":
        for u in range(UNITS):
            out += [("scores", u), ("probs", u)]
            if u % 4 == 3:
                out += [("mix", u // 4), ("context", u // 4)]
    else:
        out += [("bscores", n) for n in range(4 * TOK)] + [("bprobs", r) for r in range(4)]
        out += [("bmix", n) for n in range(4 * TOK)] + [("bturn", 0), ("bout", 0)]
    out += [("norm2", n) for n in range(NORM_PARTS)] + [("turn2", 0), ("logits", 0)]
    return out + [("route", n) for n in range(ROUTE_PARTS)] + [("wturn", 0)]


def steps_experts():
    out = [("begin", 0)]
    for i in range(FT):
        out += [("gate", i), ("up", i), ("cut", i), ("down", i)]
        if i % TILES_I == TILES_I - 1:
            out.append(("add", i // TILES_I))
    return out + [("end", 0)]


def takes_part(kind, eng, step, n):
    if eng not in WORK[step]:
        return False
    if eng == "pool" and step == "norm1":
        return n == 0
    if eng == "act" and step == "route":
        return n == 1
    if eng == "dve" and step == "qk":
        return kind == "A"
    if eng != "pe" and step in ("bscores", "bmix"):
        return n % 4 == 3
    return True


def order(kind, with_attention, with_experts):
    left = {e: [] for e in FLOW}
    needs = {}
    for is_expert, steps in ((True, steps_experts() if with_experts else []),
                             (False, steps_attention(kind) if with_attention else [])):
        for e in FLOW:
            mine = [s for s in steps if takes_part(kind, e, *s)]
            left[e].append(mine)
            for s in mine:
                w = needs_experts(e, *s) if is_expert else needs_attention(kind, e, *s)
                needs[(e,) + s] = [x for x in w if with_experts or x[1] != "begin"]
    total = {e: [len(l) or 1 for l in left[e]] for e in FLOW}
    done, free, out = {}, {e: 0.0 for e in FLOW}, {e: [] for e in FLOW}
    while any(any(l) for l in left.values()):
        best = None
        for e in FLOW:
            for k, steps in enumerate(left[e]):
                seen = set()
                for s in steps:
                    t = (e,) + s
                    if s[0] not in seen and all(w in done for w in needs[t]):
                        start = max([free[e]] + [done[w] + (HAND_OVER if w[0] != e else OWN) for w in needs[t]])
                        key = (start, -len(steps) / total[e][k])
                        if best is None or key < best[0]:
                            best = (key, k, t, start)
                    seen.add(s[0])
        _, k, t, start = best
        e, s = t[0], t[1:]
        left[e][k].remove(s)
        free[e] = done[t] = start + WORK[s[0]][e]
        out[e].append((k == 0,) + s)
    return out, max(free.values()), free


ALONE = {k: order(k, True, False) for k in "AB"}
EXPERTS_ALONE = order("A", False, True)
BESIDE = {k: order(k, True, True) for k in "AB"}

def run_passes(engine, name, attention, experts):
    for kind in "AB":
        for _, step, n in ALONE[kind][0][name]:
            attention(Pass(kind, 0), step, n)
        with engine.Fori(0, PASSES - 1) as i:
            this, following = Pass(kind, i), Pass(kind, i + 1)
            for is_expert, step, n in BESIDE[kind][0][name]:
                if is_expert:
                    experts(this, step, n)
                else:
                    attention(following, step, n)
        for _, step, n in EXPERTS_ALONE[0][name]:
            experts(Pass(kind, PASSES - 1), step, n)


def spread(ap, axis, n):
    ap = ap.unsqueeze(axis)
    shape = list(ap.shape)
    shape[axis] = n
    return ap.broadcast_to(shape)


def program(nc, x, wq, bq, wk, bk, wv, bv, rel, wqkv, bqkv, wo, bo, wg, wu, wd, wr, rb, const, out):
    def sb(name, shape, dt=F32):
        return nc.alloc_sbuf_tensor(name, shape, dt)

    cst = sb("cst", [P, C_KEPT])
    ident = cst[:, C_ID:C_ID + P]
    ones = sb("ones", [1, P])
    raw_b = sb("raw_b", [P, 2, P])
    proj = sb("proj", [P, 2, GROUPS * P])
    proj_v = sb("proj_v", [P, 2, P])
    proj_o = sb("proj_o", [P, P])
    bcol = sb("bcol", [P, 4 * GROUPS])
    bc = sb("bc", [P, 3 * P + 8])
    router = sb("router", [P, 8])
    w_hi = [sb(f"w{n}_hi", [P, EXPERTS * INNER], F32R) for n in "gu"]
    w_lo = [sb(f"w{n}_lo", [P, EXPERTS * INNER], F32R) for n in "gu"]
    wd_hi = sb("wd_hi", [P, FT, P], F32R)
    wd_lo = sb("wd_lo", [P, FT, P], F32R)
    big = sb("big", [P, HEADS * 3 * P])
    bias_a = big[:, :].rearrange("p (h y) -> p h y", h=HEADS)
    qb = big[:, 0:GROUPS * CHUNK].rearrange("p (g t) -> p g t", g=GROUPS)
    kb = big[:, GROUPS * CHUNK:2 * GROUPS * CHUNK].rearrange("p (g t) -> p g t", g=GROUPS)

    xin = sb("xin", [P, TOK, D])
    xn = sb("xn", [P, TOK, D])
    xnT = sb("xnT", [P, CHUNK])
    stats = sb("stats", [P, TOK, 6])
    moments = sb("moments", [P, TOK, 2])
    rs = sb("rs", [P, 4, TOK])
    shifted = sb("shifted", [P, 2, CHUNK])
    high = sb("high", [P, CHUNK], F32R)
    qx = sb("qx", [P, GROUPS, CHUNK], F32R)
    kx = sb("kx", [P, GROUPS, CHUNK], F32R)
    vx = sb("vx", [P, TOK, HEADS * VW + 32 - VW])
    z = sb("z", [P, Z_RING, 2 * SEQ])
    nm = sb("nm", [P, NM_RING, 2])
    probT = sb("probT", [P, PT_RING, 2 * SEQ])
    oT = sb("oT", [P, 2, SEQ])
    rec = sb("rec", [P, HEADS])
    ctxt = sb("ctxt", [P, 2, 4, DH])
    h1 = sb("h1", [P, TOK, D])
    xf = sb("xf", [P, CHUNK])
    lg = sb("lg", [P, TOK, 8])
    top = sb("top", [P, TOK, 8])
    at = sb("at", [P, TOK, 8], U32)
    atf = sb("atf", [P, TOK, 8])
    gap = sb("gap", [P, TOK])
    e2 = sb("e2", [P, TOK])
    share = sb("share", [P, 3, TOK])
    wtok = sb("wtok", [P, 3, TOK, 8])
    wts = sb("wts", [8, CHUNK])
    maxb = sb("maxb", [P, 4, HEADS])
    ctxb = xn
    ctxT = xnT
    B_BANKS = (("S0", GROUPS), ("S1", GROUPS), ("T", 2), ("O", 0))

    xh = sb("xh", [P, CHUNK], F32R)
    xl = sb("xl", [P, CHUNK], F32R)
    hid_hi = sb("hid_hi", [P, CUT_RING, CHUNK], F32R)
    hid_lo = sb("hid_lo", [P, CUT_RING, CHUNK], F32R)
    work = sb("work", [P, PIECES * STAGE])
    stage = work[:, :].rearrange("p (s c) -> p s c", s=PIECES)
    slot = work[:, :].rearrange("p (s c) -> p s c", c=CHUNK)
    th = slot[:, 0:2, :]
    hid = slot[:, 2:4, :]
    wbS, part, acc = slot[:, 4, :], slot[:, 5, :], slot[:, 6, :]
    h1F = slot[:, 7, :].rearrange("p (t d) -> p t d", t=TOK)
    xo = slot[:, 8, :].rearrange("p (t d) -> p t d", t=TOK)

    raw_a = z[:, 0, 0:2 * P].rearrange("p (m c) -> p m c", m=2)
    row_bc = z[0:1, 1, 0:3 * P + 8]
    trev = z[0:HEADS, 2, :]
    relb = z[0:BUCKETS, 3, 0:HEADS]
    row_raw = oT[0:1, :, :].rearrange("p a b -> p (a b)").rearrange("p (m c) -> p m c", m=4)
    row_rep = probT[0:1, 0:4, :]
    hot = stage[0:BUCKETS, 2, 0:512]
    flip = stage[:, 2, 512 + 7 * P:512 + 8 * P]

    BANKS = ("S0", "S1", "T", "O", "E0", "E1", "E2", "Y")
    bank = {n: nc.alloc_psum_tensor(f"bank_{n}", [P, 512], F32) for n in BANKS}

    trev_dram = nc.dram_tensor("trev_dram", [HEADS, 512], F32).ap()
    x2 = nc.dram_tensor("x2", [BATCH * SEQ, D], F32).ap()
    wts_dram = nc.dram_tensor("wts_dram", [2 * PASSES, 8, CHUNK], F32).ap()

    sem = nc.alloc_semaphore
    w_landed, row_landed, rel_landed = sem("w_landed"), sem("row_landed"), sem("rel_landed")
    trev_stored, bias_landed = sem("trev_stored"), sem("bias_landed")
    flipped, bias_ready = sem("flipped"), sem("bias_ready")
    piece_landed = [sem(f"piece_landed_{k}") for k in range(2 * PIECES)]
    x_landed, stored = sem("x_landed"), sem("stored")
    setup_dve, setup_pe, proj_b_ready = sem("setup_dve"), sem("setup_pe"), sem("proj_b_ready")
    halved, high_cut, pieces_cut = sem("halved"), sem("high_cut"), sem("pieces_cut")
    filled = {n: sem(f"filled_{n}") for n in ("S0", "S1", "T", "O", "Y")}
    emptied = {n: sem(f"emptied_{n}") for n in ("S0", "S1", "T", "O", "Y")}
    normed1, kept, qk_ready, exp_done = sem("normed1"), sem("kept"), sem("qk_ready"), sem("exp_done")
    turned, h1_part, normed2 = sem("turned"), sem("h1_part"), sem("normed2")
    gap_ready, e2_ready, routed, vstep = sem("gap_ready"), sem("e2_ready"), sem("routed"), sem("vstep")
    wts_ready, wts_stored, weight_landed = sem("wts_ready"), sem("wts_stored"), sem("weight_landed")
    xh_ready, xl_ready, h1F_ready = sem("xh_ready"), sem("xl_ready"), sem("h1F_ready")
    gate_done, up_done = sem("gate_done"), sem("up_done")
    th_ready, a_ready, h_ready = sem("th_ready"), sem("a_ready"), sem("h_ready")
    hh_ready, hl_ready, down_done = sem("hh_ready"), sem("hl_ready"), sem("down_done")
    combined, acc_ready = sem("combined"), sem("acc_ready")

    PASS_SCORES = {"A": UNITS, "B": TOK}

    def use(p, name, n):
        return p.count({k: USES[k][name] for k in "AB"}, n + 1)

    def landed(p):
        return (p.i + 1) * 16 if p.kind == "A" else (p.i + 1) * 64 + 16 * PASSES

    passed = {}

    def alone(eng):
        if eng not in passed:
            passed[eng] = sem(f"passed_{len(passed)}")
        eng.sem_inc(passed[eng], 1)

    def last_use(p, name, back=1):
        return USES[p.kind][name] - back

    def rows_of(i):
        return P if i % TILES_I < TILES_I - 1 else INNER - P * (TILES_I - 1)

    def cols_of(i):
        lo = (i // TILES_I) * INNER + (i % TILES_I) * P
        return slice(lo, lo + rows_of(i))

    def head_cols(ap, copies):
        return ap.rearrange("p (h r d) -> p h r d", h=HEADS, r=copies)

    def product_bank(m):
        return bank[("E0", "E1", "E2")[m % 3]]

    def positions(rows, i, j):
        v = rows.rearrange("(l c t j) d -> j l c t d", l=BATCH, c=PASSES, t=TOK)[j]
        return v[:, bass.ds(i, 1), :, :].rearrange("l a t d -> l (a t) d")

    def turned_out(eng, copy, p, n):
        eng.wait_ge(filled["T"], use(p, "T", 2 + n))
        eng.wait_ge(filled["O"], use(p, "O", 2 * ((n - PT_RING) // 4)))
        copy(probT[:, n % PT_RING, :], bank["T"][:, :]).then_inc(emptied["T"], 1)

    with nc.Block() as block:
        @block.sync
        def _(sp):
            sp.sem_inc(stored, 16)
            sp.dma_start(cst[:, :], const[:, 0:C_KEPT]).then_inc(w_landed, 16)
            sp.dma_start(hot, const[0:BUCKETS, C_HOT:C_HOT + 512]).then_inc(w_landed, 16)
            sp.dma_start(flip, const[:, C_FLIP:C_ALL]).then_inc(w_landed, 16)
            sp.dma_start(relb, rel).then_inc(w_landed, 16)
            sp.dma_start(raw_a[:, 0, :], wq).then_inc(w_landed, 16)
            sp.dma_start(raw_a[:, 1, :], wk).then_inc(w_landed, 16)
            sp.dma_start(row_raw[:, 0, :], bq).then_inc(row_landed, 16)
            sp.dma_start(row_raw[:, 1, :], bk).then_inc(row_landed, 16)
            sp.dma_start(row_raw[:, 2:4, :], bqkv[:, 0:2, :]).then_inc(row_landed, 16)
            sp.wait_ge(setup_dve, 3)
            sp.dma_start(row_bc[:, 0:P], bv).then_inc(row_landed, 16)
            sp.dma_start(row_bc[:, P:2 * P], bqkv[:, 2, :]).then_inc(row_landed, 16)
            sp.dma_start(row_bc[:, 2 * P:3 * P], bo).then_inc(row_landed, 16)
            sp.dma_start(row_bc[:, 3 * P:3 * P + 7], rb).then_inc(row_landed, 16)
            sp.dma_start(router[:, 0:7], wr).then_inc(row_landed, 16)

            def load(p):
                sp.wait_ge(normed1, p.count(same(1), 0))
                sp.wait_ge(kept, p.count(same(1), 0))
                if p.kind == "A":
                    src = x[bass.ds(p.i * CHUNK, CHUNK), :].rearrange("(t p) d -> p t d", p=P)
                    sp.dma_start(xin[:, :, :], src).then_inc(x_landed, 16)
                    return
                if isinstance(p.i, int):
                    sp.wait_ge(stored, 16 * (PASSES + 1))
                for j in range(4):
                    sp.dma_start(xin[32 * j:32 * j + 32, :, :], positions(x2, p.i, j)).then_inc(x_landed, 16)

            def keep_weights(p):
                sp.wait_ge(emptied["T"], use(p, "T", last_use(p, "T")))
                sp.dma_start(of_pass(p), wts[:, :]).then_inc(wts_stored, 16)

            def spread_weights(p):
                sp.wait_ge(wts_stored, 16 * p.g + 16)
                for n in range(1, EXPERTS):
                    sp.wait_ge(combined, p.count(same(EXPERTS), n))
                    row = of_pass(p)[n - 1:n, :]
                    sp.dma_start(wbS, bass.AP(row.tensor, row.offset, [[0, P], [1, CHUNK]])
                                 ).then_inc(weight_landed, 16)

            def of_pass(p):
                return wts_dram[bass.ds(p.g, 1), :, :].rearrange("a e t -> (a e) t")

            load(Pass("A", 0))
            sp.dma_start(proj_v[:, 0, :], wv).then_inc(rel_landed, 16)
            sp.dma_start(proj_v[:, 1, :], wqkv[2]).then_inc(rel_landed, 16)
            sp.dma_start(proj_o[:, :], wo).then_inc(rel_landed, 16)
            sp.dma_start(raw_b[:, :, :], wqkv[0:2].rearrange("c e i -> e c i")).then_inc(rel_landed, 16)
            sp.wait_ge(setup_dve, 11)
            sp.dma_start(trev_dram, trev).then_inc(trev_stored, 16)
            sp.wait_ge(trev_stored, 16)
            skewed = bass.AP(trev_dram.tensor, trev_dram.offset, [[1, P], [512, HEADS], [1, 3 * P]])
            sp.dma_start(bias_a, skewed).then_inc(bias_landed, 16)
            half = EXPERTS // 2
            for k in range(2 * PIECES):
                if k == 2:
                    sp.wait_ge(flipped, HEADS)
                if k >= PIECES:
                    sp.wait_ge(pieces_cut, k - PIECES + 1)
                e = (k % 2) * half
                if k < 4:
                    src = (wg, wu)[k // 2][:, e:e + half, :]
                    dst = stage[:, k % PIECES, 0:half * INNER].rearrange("p (e c) -> p e c", e=half)
                    sp.dma_start(dst, src).then_inc(piece_landed[k], 16)
                else:
                    src = wd[e:e + half].rearrange("e (t p) h -> p (e t) h", p=P)
                    dst = stage[:, k % PIECES, :].rearrange("p (c h) -> p c h", h=P)
                    sp.dma_start(dst, src).then_inc(piece_landed[k], 16)
            for kind in "AB":
                if kind == "B":
                    load(Pass("B", 0))
                keep_weights(Pass(kind, 0))
                with sp.Fori(0, PASSES - 1) as i:
                    load(Pass(kind, i + 1))
                    spread_weights(Pass(kind, i))
                    keep_weights(Pass(kind, i + 1))
                spread_weights(Pass(kind, PASSES - 1))
            sp.wait_ge(wts_stored, 16 * 2 * PASSES)
            sp.wait_ge(stored, 16 * (1 + PASSES + 4 * PASSES))

        @block.gpsimd
        def _(pool):
            for s in (kept, hl_ready, h1F_ready, acc_ready):
                pool.sem_inc(s, CREDIT)

            def keep(p):
                pool.wait_ge(x_landed, landed(p))
                pool.wait_ge(normed2, p.count(same(1), 0))
                pool.wait_ge(h1F_ready, p.count(same(1), 0))
                alone(pool)
                if p.kind == "A":
                    pool.tensor_copy(h1[:, :, :], xin[:, :, :]).then_inc(kept, 1)
                else:
                    pool.tensor_tensor(h1[:, :, :], xin[:, :, :], spread(bc[:, 2 * P:3 * P], 1, TOK),
                                       ALU.add).then_inc(kept, 1)

            def attention(p, step, n):
                if step == "norm1" and n == 0:
                    keep(p)

            def experts(p, step, n):
                if step == "begin":
                    if p.kind == "A":
                        pool.wait_ge(h1_part, p.count({"A": 2 * GROUPS, "B": 0}, 2 * GROUPS))
                    else:
                        pool.wait_ge(emptied["S0"], use(p, "S0", last_use(p, "S0")))
                    pool.wait_ge(emptied["Y"], p.count(same(1), 0))
                    alone(pool)
                    pool.tensor_copy(h1F, h1[:, :, :]).then_inc(h1F_ready, 1)
                elif step == "cut":
                    r = rows_of(n)
                    pool.wait_ge(hh_ready, p.count(same(FT), n + 1))
                    pool.wait_ge(down_done, p.count(same(FT), n + 1 - CUT_RING))
                    pool.tensor_tensor(hid_lo[0:r, n % CUT_RING, :], hid[0:r, n % H_RING, :],
                                       hid_hi[0:r, n % CUT_RING, :].bitcast(F32), ALU.subtract).then_inc(hl_ready, 1)
                elif step == "add" and n > 0:
                    pool.wait_ge(combined, p.count(same(EXPERTS), n + 1))
                    if n > 1:
                        pool.wait_ge(acc_ready, p.count(same(EXPERTS - 1), n - 1))
                    pool.tensor_tensor(acc, acc, part, ALU.add).then_inc(acc_ready, 1)

            first = Pass("A", 0)
            keep(first)
            for k in range(2 * PIECES):
                pool.wait_ge(piece_landed[k], 16)
                if k < 4:
                    width = (EXPERTS // 2) * INNER
                    lo = (k % 2) * width
                    raw = stage[:, k % PIECES, 0:width]
                    hi_dst, lo_dst = w_hi[k // 2][:, lo:lo + width], w_lo[k // 2][:, lo:lo + width]
                else:
                    raw = stage[:, k % PIECES, :]
                    part_of = slice((k % 2) * FT // 2, (k % 2 + 1) * FT // 2)
                    hi_dst = wd_hi[:, part_of, :].rearrange("p c h -> p (c h)")
                    lo_dst = wd_lo[:, part_of, :].rearrange("p c h -> p (c h)")
                    pool.tensor_scalar(raw, raw, 0.5, None, ALU.mult).then_inc(halved, 1)
                    pool.wait_ge(halved, k - 3)
                pool.tensor_copy(hi_dst, raw).then_inc(high_cut, 1)
                pool.wait_ge(high_cut, k + 1)
                pool.tensor_tensor(lo_dst, raw, hi_dst.bitcast(F32), ALU.subtract).then_inc(pieces_cut, 1)
            pool.wait_ge(pieces_cut, 2 * PIECES)

            def attention_but_first(p, step, n):
                if p.kind == "B" or not isinstance(p.i, int):
                    attention(p, step, n)

            run_passes(pool, "pool", attention_but_first, experts)

        @block.scalar
        def _(act):
            for h in range(HEADS):
                act.wait_ge(flipped, h + 1)
                act.activation(bias_a[:, h, :], bank[("E0", "E1", "E2", "Y")[h % 4]][:, 0:3 * P], ACT.Copy).then_inc(bias_ready, 1)
            for s in (exp_done, th_ready, hh_ready, e2_ready):
                act.sem_inc(s, CREDIT)

            def attention(p, step, n):
                if step == "turn1":
                    act.wait_ge(filled["T"], use(p, "T", 0))
                    act.activation(xnT[:, :], bank["T"][:, :], ACT.Copy).then_inc(emptied["T"], 1)
                elif step == "qk":
                    s, g, m = f"S{n % 2}", n // 2, n % 2
                    act.wait_ge(filled[s], use(p, s, g))
                    if p.kind == "A":
                        act.wait_ge(qk_ready, p.count({"A": 2 * GROUPS, "B": 0}, n - 1))
                        dst, b = shifted[:, m, :], bcol[:, m * GROUPS + g:m * GROUPS + g + 1]
                    else:
                        dst, b = (qb, kb)[m][:, g, :], bcol[:, (2 + m) * GROUPS + g:(2 + m) * GROUPS + g + 1]
                    act.activation(dst, bank[s][:, :], ACT.Identity, bias=b).then_inc(emptied[s], 1)
                elif step == "scores":
                    act.wait_ge(emptied[f"S{n % 2}"], use(p, f"S{n % 2}", GROUPS + n // 2))
                    for t in range(2):
                        zt = z[:, n % Z_RING, t * SEQ:(t + 1) * SEQ]
                        last = act.activation(zt, zt, ACT.Exp, bias=nm[:, n % NM_RING, t:t + 1], scale=-1.0)
                    last.then_inc(exp_done, 1)
                elif step == "probs":
                    turned_out(act, act.copy, p, n)
                elif step == "bscores":
                    n = n // 4
                    s, k = B_BANKS[n]
                    act.wait_ge(emptied[s], use(p, s, k))
                    act.activation(z[:, n, :], z[:, n, :], ACT.Exp).then_inc(exp_done, 1)
                elif step == "bturn":
                    act.wait_ge(filled["T"], use(p, "T", 3))
                    act.activation(ctxT[:, :], bank["T"][:, :], ACT.Copy).then_inc(emptied["T"], 1)
                elif step == "turn2":
                    act.wait_ge(filled["T"], use(p, "T", last_use(p, "T", 3)))
                    act.wait_ge(xl_ready, p.count(same(1), 0))
                    act.activation(xf[:, :], bank["T"][:, :], ACT.Copy).then_inc(emptied["T"], 1)
                elif step == "route" and n == 1:
                    act.wait_ge(gap_ready, p.count(same(1), 1))
                    act.activation(e2[:, :], gap[:, :], ACT.Exp).then_inc(e2_ready, 1)

            def experts(p, step, n):
                if step == "end":
                    act.wait_ge(emptied["Y"], p.count(same(1), 1))
                    if p.kind == "A":
                        dst = x2[bass.ds(p.i * CHUNK, CHUNK), :].rearrange("(t p) d -> p t d", p=P)
                        act.dma_start(dst, xo).then_inc(stored, 16)
                    else:
                        for j in range(4):
                            act.dma_start(positions(out, p.i, j), xo[32 * j:32 * j + 32, :, :]).then_inc(stored, 16)
                elif step == "gate":
                    r = rows_of(n)
                    act.wait_ge(gate_done, p.count(same(FT), n + 1))
                    act.wait_ge(h_ready, p.count(same(FT), n - 1))
                    act.activation(th[0:r, n % 2, :], product_bank(2 * n)[0:r, :], ACT.Tanh, scale=0.5).then_inc(th_ready, 1)
                elif step == "cut":
                    r = rows_of(n)
                    act.wait_ge(h_ready, p.count(same(FT), n + 1))
                    act.wait_ge(down_done, p.count(same(FT), n + 1 - CUT_RING))
                    act.activation(hid_hi[0:r, n % CUT_RING, :], hid[0:r, n % H_RING, :], ACT.Copy
                                   ).then_inc(hh_ready, 1)

            passes = [attention, experts]

            def experts_after_cuts(p, step, n):
                if step == "begin" and p.kind == "A":
                    act.wait_ge(pieces_cut, 2 * PIECES)
                passes[1](p, step, n)

            act.wait_ge(setup_dve, 13)
            run_passes(act, "act", attention, experts_after_cuts)

        @block.vector
        def _(dve):
            for s in (emptied["S0"], emptied["S1"], emptied["T"], emptied["O"], emptied["Y"], normed1, qk_ready,
                      turned, h1_part, normed2, gap_ready, routed, xh_ready, xl_ready,
                      a_ready, h_ready, combined):
                dve.sem_inc(s, CREDIT)
            dve.memset(ones[:, :], 1.0).then_inc(setup_dve, 1)
            dve.memset(row_bc[:, 3 * P:3 * P + 8], -FAR).then_inc(setup_dve, 1)
            dve.memset(router[:, :], 0.0).then_inc(setup_dve, 1)
            dve.memset(vx[:, :, :], 1.0).then_inc(setup_dve, 1)
            dve.wait_ge(w_landed, 6 * 16)
            dve.tensor_scalar(head_cols(proj[:, 0, :], 4), spread(raw_a[:, 0, :].rearrange("p (h d) -> p h d", h=HEADS), 2, 4),
                              SCALE, None, ALU.mult).then_inc(setup_dve, 1)
            dve.tensor_copy(head_cols(proj[:, 1, :], 4), spread(raw_a[:, 1, :].rearrange("p (h d) -> p h d", h=HEADS), 2, 4)
                            ).then_inc(setup_dve, 1)
            dve.wait_ge(row_landed, 8 * 16)
            for m in range(4):
                src = spread(row_raw[:, m, :].rearrange("p (h d) -> p h d", h=HEADS), 2, 4)
                dve.tensor_scalar(head_cols(row_rep[:, m, :], 4), src, SCALE if m % 2 == 0 else 1.0, None,
                                  ALU.mult).then_inc(setup_dve, 1)
            dve.wait_ge(setup_pe, 1)
            dve.tensor_copy(trev, bank["O"][0:HEADS, :]).then_inc(setup_dve, 1)
            dve.wait_ge(setup_pe, 2)
            dve.tensor_copy(bcol[:, :], bank["S0"][:, 0:4 * GROUPS]).then_inc(setup_dve, 1)
            dve.wait_ge(setup_pe, 3)
            dve.tensor_copy(bc[:, :], bank["T"][:, 0:3 * P + 8]).then_inc(setup_dve, 1)

            steps = [0]

            def then(p, instruction):
                mark(instruction)
                settle()

            def mark(instruction):
                steps[0] += 1
                instruction.then_inc(vstep, 1)

            def settle():
                dve.wait_ge(vstep, steps[0])

            def normalise(p, rows, done, n):
                v, y, a, b = (rs[:, k, :] for k in range(4))
                if n > 0:
                    settle()
                if n == 0:
                    for t in range(TOK):
                        last = dve.bn_stats(stats[:, t, :], rows[:, t, :])
                    mark(last)
                elif n == 1:
                    for t in range(TOK):
                        last = dve.bn_aggr(moments[:, t, :], stats[:, t, :])
                    mark(last)
                elif n == 2:
                    then(p, dve.tensor_scalar(v, moments[:, :, 1], EPS, None, ALU.add))
                    mark(dve.tensor_scalar(y.bitcast(I32), v.bitcast(I32), -0.5, MAGIC, ALU.mult, ALU.add))
                elif n < NORM_PARTS - 1:
                    then(p, dve.scalar_tensor_tensor(out=a, in0=y, scalar=-0.5, in1=y, op0=ALU.mult, op1=ALU.mult))
                    then(p, dve.tensor_tensor(b, a, v, ALU.mult))
                    mark(dve.scalar_tensor_tensor(out=y, in0=b, scalar=1.5, in1=y, op0=ALU.add, op1=ALU.mult))
                else:
                    for t in range(TOK):
                        last = dve.tensor_scalar(xn[:, t, :], rows[:, t, :], moments[:, t, 0:1], y[:, t:t + 1],
                                                 ALU.subtract, ALU.mult)
                    last.then_inc(done, 1)

            def route(p, n):
                s, first, second = (share[:, k, :] for k in range(3))
                settle()
                if n == 0:
                    for t in range(TOK):
                        last = dve.max(top[:, t, :], lg[:, t, :])
                    mark(last)
                elif n == 1:
                    for t in range(TOK):
                        last = dve.max_index(at[:, t, :], top[:, t, :], lg[:, t, :])
                    mark(last)
                    dve.tensor_tensor(gap[:, :], top[:, :, 1], top[:, :, 0], ALU.subtract).then_inc(gap_ready, 1)
                elif n == 2:
                    mark(dve.tensor_copy(atf[:, :, :], at[:, :, :]))
                elif n == 3:
                    dve.wait_ge(e2_ready, p.count(same(1), 1))
                    then(p, dve.tensor_scalar(s, e2[:, :], 1.0, None, ALU.add))
                    then(p, dve.reciprocal(first, s))
                    mark(dve.tensor_tensor(second, e2[:, :], first, ALU.mult))
                elif n == 4:
                    for t in range(TOK):
                        for k, w in enumerate((first, second)):
                            last = dve.tensor_scalar(wtok[:, k, t, :], cst[:, C_IOTA:C_IOTA + 8], atf[:, t, k:k + 1],
                                                     w[:, t:t + 1], ALU.is_equal, ALU.mult)
                    then(p, last)
                    dve.tensor_tensor(wtok[:, 2, :, :], wtok[:, 0, :, :], wtok[:, 1, :, :], ALU.add).then_inc(routed, 1)

            def attention(p, step, n):
                if step == "norm1":
                    if n == 0:
                        steps[0] = 1
                        dve.sem_clear(vstep)
                        dve.sem_inc(vstep, 1)
                        dve.wait_ge(x_landed, landed(p))
                    normalise(p, xin, normed1, n)
                elif step == "qk" and p.kind == "A":
                    s, g, m = f"S{n % 2}", n // 2, n % 2
                    dve.wait_ge(emptied[s], use(p, s, g))
                    dve.wait_ge(qk_ready, p.count({"A": 2 * GROUPS, "B": 0}, n))
                    then(p, dve.tensor_copy(high[:, :], shifted[:, m, :]))
                    mask = cst[:, C_MQ + m:C_MQ + m + 1]
                    dve.scalar_tensor_tensor(out=(qx, kx)[m][:, g, :], in0=high[:, :].bitcast(F32), scalar=mask,
                                             in1=shifted[:, m, :], op0=ALU.mult, op1=ALU.add).then_inc(qk_ready, 1)
                elif step == "v":
                    m = "AB".index(p.kind)
                    dve.wait_ge(filled["T"], use(p, "T", 1))
                    dst = vx[:, :, 0:HEADS * VW].rearrange("p t (h c) -> p t h c", c=VW)[:, :, :, 0:DH]
                    src = bank["T"][:, :].rearrange("p (t h d) -> p t h d", t=TOK, d=DH)
                    b = spread(bc[:, m * P:(m + 1) * P].rearrange("p (h d) -> p h d", d=DH), 1, TOK)
                    dve.tensor_tensor(dst, src, b, ALU.add).then_inc(emptied["T"], 1)
                elif step == "scores":
                    s, h = f"S{n % 2}", n % HEADS
                    if n == 0:
                        dve.wait_ge(bias_ready, HEADS)
                    dve.wait_ge(filled[s], use(p, s, GROUPS + n // 2))
                    dve.wait_ge(filled["T"], use(p, "T", 2 + n - Z_RING))
                    alone(dve)
                    for t in range(2):
                        last = dve.tensor_tensor_reduce(
                            z[:, n % Z_RING, t * SEQ:(t + 1) * SEQ], bank[s][:, t * SEQ:(t + 1) * SEQ],
                            bias_a[:, h, P - P * t:P - P * t + SEQ], -1.0, FAR, ALU.add, ALU.min,
                            nm[:, n % NM_RING, t:t + 1])
                    last.then_inc(emptied[s], 1)
                elif step == "mix":
                    dve.wait_ge(filled["O"], use(p, "O", 2 * n))
                    dve.tensor_copy(oT[:, n % 2, :], bank["O"][:, 0:SEQ]).then_inc(emptied["O"], 1)
                elif step == "context":
                    dve.wait_ge(filled["O"], use(p, "O", 2 * n + 1))
                    o = bank["O"][:, 0:SEQ].rearrange("p (t j c) -> p (t j) c", t=2, j=4)
                    c8 = ctxt[:, :, :, :].rearrange("p t j d -> p (t j) d")
                    then(p, dve.reciprocal(rec[:, 0:8], o[:, :, DH]))
                    dve.tensor_tensor(c8, o[:, :, 0:DH], spread(rec[:, 0:8], 2, DH), ALU.mult).then_inc(emptied["O"], 1)
                    dve.wait_ge(emptied["O"], use(p, "O", 2 * n + 1))
                    dve.wait_ge(kept, p.count(same(1), 1))
                    b, g = n // GROUPS, n % GROUPS
                    dst = h1[:, 2 * b:2 * b + 2, 32 * g:32 * g + 32]
                    dve.tensor_tensor(dst, dst, ctxt[:, :, :, :].rearrange("p t j d -> p t (j d)"), ALU.add
                                      ).then_inc(h1_part, 1)
                elif step == "bscores":
                    n = n // 4
                    s, k = B_BANKS[n]
                    dve.wait_ge(filled[s], use(p, s, k))
                    sc = bank[s][:, :].rearrange("p (h m) -> p h m", m=32)
                    then(p, dve.tensor_reduce(maxb[:, n, :], sc, AX.X, ALU.max))
                    dve.wait_ge(turned, p.count({"A": 0, "B": 4}, n - 3))
                    dve.tensor_tensor(z[:, n, :].rearrange("p (h m) -> p h m", m=32), sc,
                                      spread(maxb[:, n, :], 2, 32), ALU.subtract).then_inc(emptied[s], 1)
                elif step == "bprobs":
                    dve.wait_ge(exp_done, p.count(PASS_SCORES, n + 1))
                    dve.transpose(probT[:, n, :], z[:, n, :]).then_inc(turned, 1)
                elif step == "bmix":
                    n = n // 4
                    dve.wait_ge(filled["O"], use(p, "O", 1 + n))
                    o = bank["O"][:, 0:HEADS * VW].rearrange("p (h c) -> p h c", c=VW)
                    then(p, dve.reciprocal(rec[:, :], o[:, :, DH]))
                    dve.tensor_tensor(ctxb[:, n, :].rearrange("p (h d) -> p h d", d=DH), o[:, :, 0:DH],
                                      spread(rec[:, :], 2, DH), ALU.mult).then_inc(emptied["O"], 1)
                elif step == "bout":
                    dve.wait_ge(filled["S0"], use(p, "S0", last_use(p, "S0")))
                    dve.wait_ge(kept, p.count(same(1), 1))
                    o = bank["S0"][:, :].rearrange("p (t d) -> p t d", t=TOK)
                    dve.tensor_tensor(h1[:, :, :], h1[:, :, :], o, ALU.add).then_inc(emptied["S0"], 1)
                elif step == "norm2":
                    if n == 0 and p.kind == "A":
                        dve.wait_ge(h1_part, p.count({"A": 2 * GROUPS, "B": 0}, 2 * GROUPS))
                    elif n == 0:
                        dve.wait_ge(emptied["S0"], use(p, "S0", last_use(p, "S0")))
                    normalise(p, h1, normed2, n)
                elif step == "logits":
                    dve.wait_ge(filled["T"], use(p, "T", last_use(p, "T", 2)))
                    dve.tensor_tensor(lg[:, :, :], bank["T"][:, 0:8 * TOK].rearrange("p (t e) -> p t e", t=TOK),
                                      spread(bc[:, 3 * P:3 * P + 8], 1, TOK), ALU.add).then_inc(emptied["T"], 1)
                    dve.wait_ge(emptied["T"], use(p, "T", last_use(p, "T", 2)))
                    alone(dve)
                elif step == "route":
                    route(p, n)
                elif step == "wturn":
                    dve.wait_ge(filled["T"], use(p, "T", last_use(p, "T")))
                    if not (p.kind == "A" and isinstance(p.i, int)):
                        dve.wait_ge(wts_stored, 16 * p.g)
                    dve.tensor_copy(wts[:, :], bank["T"][0:8, :]).then_inc(emptied["T"], 1)

            def experts(p, step, n):
                if step == "begin":
                    if p.kind == "A":
                        dve.wait_ge(pieces_cut, 2 * PIECES)
                    dve.wait_ge(filled["Y"], p.count(same(1), 0))
                    dve.wait_ge(emptied["T"], use(p, "T", last_use(p, "T")))
                    dve.tensor_copy(xh[:, :], xf[:, :]).then_inc(xh_ready, 1)
                    dve.wait_ge(xh_ready, p.count(same(1), 1))
                    dve.tensor_tensor(xl[:, :], xf[:, :], xh[:, :].bitcast(F32), ALU.subtract).then_inc(xl_ready, 1)
                elif step == "gate":
                    r = rows_of(n)
                    dve.wait_ge(th_ready, p.count(same(FT), n + 1))
                    a = th[0:r, n % 2, :]
                    dve.scalar_tensor_tensor(out=a, in0=a, scalar=1.0, in1=product_bank(2 * n)[0:r, :], op0=ALU.add,
                                             op1=ALU.mult).then_inc(a_ready, 1)
                elif step == "up":
                    r = rows_of(n)
                    dve.wait_ge(a_ready, p.count(same(FT), n + 1))
                    dve.wait_ge(up_done, p.count(same(FT), n + 1))
                    dve.wait_ge(hl_ready, p.count(same(FT), n + 1 - H_RING))
                    dve.tensor_tensor(hid[0:r, n % H_RING, :], th[0:r, n % 2, :], product_bank(2 * n + 1)[0:r, :], ALU.mult
                                      ).then_inc(h_ready, 1)
                elif step == "add":
                    dve.wait_ge(down_done, p.count(same(FT), TILES_I * (n + 1)))
                    if n == 0:
                        dve.wait_ge(filled["Y"], p.count(same(1), 0))
                        dve.tensor_copy(acc, bank["Y"][:, :]).then_inc(combined, 1)
                    else:
                        dve.wait_ge(weight_landed, 16 * (p.g * (EXPERTS - 1) + n))
                        dve.wait_ge(acc_ready, p.count(same(EXPERTS - 1), n - 1))
                        dve.tensor_tensor(part, bank["Y"][:, :], wbS, ALU.mult).then_inc(combined, 1)
                elif step == "end":
                    dve.wait_ge(filled["Y"], p.count(same(1), 1))
                    dve.wait_ge(h1F_ready, p.count(same(1), 1))
                    dve.wait_ge(stored, p.i * 16 + 16 if p.kind == "A" else p.i * 64 + 16 * (PASSES + 1))
                    dve.tensor_tensor(xo, bank["Y"][:, :].rearrange("p (t d) -> p t d", t=TOK), h1F, ALU.add
                                      ).then_inc(emptied["Y"], 1)

            def with_weights(p, step, n):
                if p.kind == "B" and isinstance(p.i, int) and step == "norm1" and n == 0:
                    dve.wait_ge(rel_landed, 4 * 16)
                    for m in range(2):
                        src = spread(raw_b[:, m, :].rearrange("p (h d) -> p h d", h=HEADS), 2, 4)
                        dve.tensor_scalar(head_cols(proj[:, m, :], 4), src, 1.0 if m else SCALE, None, ALU.mult
                                          ).then_inc(proj_b_ready, 1)
                attention(p, step, n)

            run_passes(dve, "dve", with_weights, experts)

        @block.tensor
        def _(pe):
            for s in list(filled.values()) + [gate_done, up_done, down_done]:
                pe.sem_inc(s, CREDIT)
            pe.wait_ge(w_landed, 6 * 16)
            pe.matmul(bank["O"][0:HEADS, :], relb, hot, start=True, stop=True).then_inc(setup_pe, 1)
            pe.wait_ge(setup_dve, 10)
            for m in range(4):
                for g in range(GROUPS):
                    c = m * GROUPS + g
                    last = pe.matmul(bank["S0"][:, c:c + 1], row_rep[:, m, g * P:(g + 1) * P], ones[:, 0:1],
                                     start=True, stop=True)
            last.then_inc(setup_pe, 1)
            pe.matmul(bank["T"][:, 0:3 * P + 8], ones[:, :], row_bc, start=True, stop=True).then_inc(setup_pe, 1)
            pe.wait_ge(bias_landed, 16)
            for h in range(HEADS):
                if h >= 4:
                    pe.wait_ge(bias_ready, h - 3)
                pe.matmul(bank[("E0", "E1", "E2", "Y")[h % 4]][:, 0:3 * P], flip, bias_a[:, h, :], start=True, stop=True
                          ).then_inc(flipped, 1)
            pe.wait_ge(setup_dve, 13)
            pe.wait_ge(rel_landed, 4 * 16)

            def next_use(p, name, n):
                pe.wait_ge(emptied[name], use(p, name, n - 1))

            def turn_rows(p, rows, n):
                next_use(p, "T", n)
                for t in range(TOK):
                    last = pe.transpose(bank["T"][:, t * P:(t + 1) * P], rows[:, t, :], ident)
                last.then_inc(filled["T"], 1)

            def attention(p, step, n):
                half = "AB".index(p.kind)
                if step == "turn1":
                    pe.wait_ge(normed1, p.count(same(1), 1))
                    turn_rows(p, xn, 0)
                elif step == "qk":
                    s, g, m = f"S{n % 2}", n // 2, n % 2
                    pe.wait_ge(emptied["T"], use(p, "T", 0))
                    if half and isinstance(p.i, int):
                        pe.wait_ge(proj_b_ready, 2)
                    next_use(p, s, g)
                    pe.matmul(bank[s][:, :], proj[:, m, g * P:(g + 1) * P], xnT[:, :], start=True, stop=True
                              ).then_inc(filled[s], 1)
                elif step == "v":
                    next_use(p, "T", 1)
                    for t in range(TOK):
                        last = pe.matmul(bank["T"][:, t * P:(t + 1) * P], xnT[:, t * P:(t + 1) * P],
                                         proj_v[:, half, :], start=True, stop=True)
                    last.then_inc(filled["T"], 1)
                elif step == "scores":
                    s, b, h = f"S{n % 2}", n // HEADS, n % HEADS
                    rows, g = slice(32 * (h % 4), 32 * (h % 4) + 32), h // 4
                    pe.wait_ge(qk_ready, p.count({"A": 2 * GROUPS, "B": 0}, 2 * GROUPS))
                    next_use(p, s, GROUPS + n // 2)
                    for t in range(2):
                        lo = b * SEQ + t * P
                        last = pe.matmul(bank[s][:, t * SEQ:(t + 1) * SEQ], qx[rows, g, lo:lo + P],
                                         kx[rows, g, b * SEQ:(b + 1) * SEQ], start=True, stop=True)
                    last.then_inc(filled[s], 1)
                elif step == "probs":
                    pe.wait_ge(exp_done, p.count(PASS_SCORES, n + 1))
                    next_use(p, "T", 2 + n)
                    for k in range(2):
                        for t in range(2):
                            c = k * SEQ + t * P
                            last = pe.transpose(bank["T"][:, c:c + P],
                                                z[:, n % Z_RING, t * SEQ + k * P:t * SEQ + (k + 1) * P], ident)
                    last.then_inc(filled["T"], 1)
                elif step == "mix":
                    pe.wait_ge(emptied["T"], use(p, "T", 2 + 4 * n + 3))
                    next_use(p, "O", 2 * n)
                    b, g = n // GROUPS, n % GROUPS
                    for k in range(2):
                        for j in range(4):
                            u, c = 4 * n + j, (4 * g + j) * VW
                            last = pe.matmul(bank["O"][32 * j:32 * j + 32, 0:SEQ], vx[:, 2 * b + k, c:c + 32],
                                             probT[:, u % PT_RING, k * SEQ:(k + 1) * SEQ], start=(k == 0),
                                             stop=(k == 1), tile_position=(0, 32 * j))
                    last.then_inc(filled["O"], 1)
                elif step == "context":
                    next_use(p, "O", 2 * n + 1)
                    for t in range(2):
                        last = pe.transpose(bank["O"][:, t * P:(t + 1) * P], oT[:, n % 2, t * P:(t + 1) * P], ident)
                    last.then_inc(filled["O"], 1)
                elif step == "bscores":
                    r, t = n // TOK, n % TOK
                    s, use_s = B_BANKS[r]
                    if t == 0:
                        for k in range(2):
                            pe.wait_ge(emptied[f"S{k}"], use(p, f"S{k}", GROUPS - 1))
                        next_use(p, s, use_s)
                        alone(pe)
                    rows = slice(32 * r, 32 * r + DH)
                    for g in range(GROUPS):
                        c = (t * GROUPS + g) * 32
                        for j in range(4):
                            lo = t * P + 32 * j
                            last = pe.matmul(bank[s][32 * j:32 * j + 32, c:c + 32], qb[rows, g, lo:lo + 32],
                                             kb[rows, g, lo:lo + 32], start=True, stop=True,
                                             tile_position=(32 * r, 32 * j))
                    if t == TOK - 1:
                        last.then_inc(filled[s], 1)
                elif step == "bmix":
                    t, g = n // GROUPS, n % GROUPS
                    if g == 0:
                        pe.wait_ge(turned, p.count({"A": 0, "B": 4}, 4))
                        next_use(p, "O", 1 + t)
                        alone(pe)
                    c = (t * GROUPS + g) * 32
                    for h in range(4 * g, 4 * g + 4):
                        for j in range(4):
                            r = slice(32 * j, 32 * j + 32)
                            last = pe.matmul(bank["O"][r, h * VW:(h + 1) * VW], probT[r, h % 4, c:c + 32],
                                             vx[r, t, h * VW:(h + 1) * VW], start=True, stop=True,
                                             tile_position=(32 * j, 32 * j))
                    if g == GROUPS - 1:
                        last.then_inc(filled["O"], 1)
                elif step == "bturn":
                    pe.wait_ge(emptied["O"], use(p, "O", TOK))
                    turn_rows(p, ctxb, 3)
                elif step == "bout":
                    pe.wait_ge(emptied["T"], use(p, "T", 3))
                    next_use(p, "S0", last_use(p, "S0"))
                    for t in range(TOK):
                        last = pe.matmul(bank["S0"][:, t * P:(t + 1) * P], ctxT[:, t * P:(t + 1) * P], proj_o[:, :],
                                         start=True, stop=True)
                    last.then_inc(filled["S0"], 1)
                elif step == "turn2":
                    pe.wait_ge(normed2, p.count(same(1), 1))
                    turn_rows(p, xn, last_use(p, "T", 3))
                elif step == "logits":
                    next_use(p, "T", last_use(p, "T", 2))
                    for t in range(TOK):
                        last = pe.matmul(bank["T"][:, 8 * t:8 * t + 8], xf[:, t * P:(t + 1) * P], router[:, :],
                                         start=True, stop=True)
                    last.then_inc(filled["T"], 1)
                elif step == "wturn":
                    pe.wait_ge(routed, p.count(same(1), 1))
                    next_use(p, "T", last_use(p, "T"))
                    for t in range(TOK):
                        last = pe.transpose(bank["T"][0:8, t * P:(t + 1) * P], wtok[:, 2, t, :], ident)
                    last.then_inc(filled["T"], 1)

            def product(dst, high_w, low_w, high_x, low_x, start=True, stop=True):
                pe.matmul(dst, high_w, high_x, start=start, stop=False)
                pe.matmul(dst, high_w, low_x, start=False, stop=False)
                return pe.matmul(dst, low_w, high_x, start=False, stop=stop)

            def experts(p, step, n):
                if step == "begin":
                    pe.wait_ge(xl_ready, p.count(same(1), 1))
                    if p.kind == "A":
                        pe.wait_ge(pieces_cut, 2 * PIECES)
                elif step == "gate":
                    r, c = rows_of(n), cols_of(n)
                    pe.wait_ge(h_ready, p.count(same(FT), n - 1))
                    product(product_bank(2 * n)[0:r, :], w_hi[0][:, c], w_lo[0][:, c], xh[:, :], xl[:, :]
                            ).then_inc(gate_done, 1)
                elif step == "up":
                    r, c = rows_of(n), cols_of(n)
                    pe.wait_ge(a_ready, p.count(same(FT), n))
                    product(product_bank(2 * n + 1)[0:r, :], w_hi[1][:, c], w_lo[1][:, c], xh[:, :], xl[:, :]
                            ).then_inc(up_done, 1)
                elif step == "down":
                    r, e, k = rows_of(n), n // TILES_I, n % TILES_I
                    pe.wait_ge(hl_ready, p.count(same(FT), n + 1))
                    if k == 0:
                        pe.wait_ge(combined, p.count(same(EXPERTS), e))
                        if e == 0:
                            pe.wait_ge(emptied["Y"], p.count(same(1), 0))
                    ins = product(bank["Y"][:, :], wd_hi[0:r, n, :], wd_lo[0:r, n, :], hid_hi[0:r, n % CUT_RING, :],
                                  hid_lo[0:r, n % CUT_RING, :], start=(k == 0), stop=(k == TILES_I - 1))
                    ins.then_inc(down_done, 1)
                elif step == "end":
                    pe.wait_ge(acc_ready, p.count(same(EXPERTS - 1), EXPERTS - 1))
                    pe.wait_ge(combined, p.count(same(EXPERTS), EXPERTS))
                    for t in range(TOK):
                        last = pe.transpose(bank["Y"][:, t * P:(t + 1) * P], acc[:, t * P:(t + 1) * P], ident)
                    last.then_inc(filled["Y"], 1)

            run_passes(pe, "pe", attention, experts)


def kernel(**inputs):
    import concourse.bacc as bacc
    from concourse.bass_utils import run_bass_kernel_spmd

    def a(name):
        return np.asarray(inputs["L0_" + name])

    row = lambda t: t.reshape(1, -1)
    inner_first = lambda shared, routed: np.concatenate([shared[None], routed]).transpose(2, 0, 1)
    down = np.concatenate([a("ffn_sd")[None], a("ffn_rd")]).transpose(0, 2, 1)
    arrays = {
        "x": a("attn_a_hidden_states").reshape(BATCH * SEQ, D),
        "wq": a("attn_a_Wq"), "bq": row(a("attn_a_bq")), "wk": a("attn_a_Wk"), "bk": row(a("attn_a_bk")),
        "wv": a("attn_a_Wv"), "bv": row(a("attn_a_bv")), "rel": a("attn_a_rel_bias"),
        "wqkv": a("attn_b_qkv_proj").reshape(P, 3, D).transpose(1, 2, 0),
        "bqkv": a("attn_b_qkv_bias").reshape(P, 3).T.reshape(1, 3, P),
        "wo": a("attn_b_out_proj").T, "bo": row(a("attn_b_out_bias")),
        "wg": inner_first(a("ffn_sg"), a("ffn_rg")), "wu": inner_first(a("ffn_su"), a("ffn_ru")),
        "wd": np.concatenate([down, np.zeros((EXPERTS, P * TILES_I - INNER, D), down.dtype)], axis=1),
        "wr": a("ffn_wr").T, "rb": row(a("ffn_rb")), "const": constants(),
    }
    arrays = {f"in_{k}": np.ascontiguousarray(v) for k, v in arrays.items()}
    nc = bacc.Bacc("TRN2", target_bir_lowering=False, num_devices=1)
    args = [nc.dram_tensor(k, v.shape, mybir.dt.from_np(v.dtype), kind="ExternalInput").ap() for k, v in arrays.items()]
    out = nc.dram_tensor("out_x", (BATCH * SEQ, D), F32, kind="ExternalOutput").ap()
    program(nc, *args, out)
    result = run_bass_kernel_spmd(nc, [arrays], core_ids=[0])
    return result.results[0]["out_x"].reshape(BATCH, SEQ, D)
```

```python
import numpy as np
import concourse.bass as bass
from concourse import mybir

F32 = mybir.dt.float32
F32R = mybir.dt.float32r
I32 = mybir.dt.int32
U32 = mybir.dt.uint32
ALU = mybir.AluOpType
ACT = mybir.ActivationFunctionType
AX = mybir.AxisListType

P = 128
BATCH, SEQ, D = 32, 256, 128
HEADS, DH = 16, 8
BUCKETS = 32
EXPERTS, INNER = 8, 352
CHUNK = 512
TOK = CHUNK // P
PASSES = BATCH * SEQ // CHUNK
GROUPS = HEADS // 4
UNITS = 2 * HEADS
FT = EXPERTS * INNER // P
SHARED_TILES = INNER // P
EPS = 1e-5
MAGIC = float(0x5F3759DF)
NEWTON = 3
FAR = 3.0e38

CREDIT = 8

Z_RING = 4
PT_RING = 5
NM_RING = 8
H_RING = 3
WB_RING = 2
CUT_RING = 3

VW = DH + 1
STAGE, PIECES = EXPERTS * INNER // 2, 3
SCALE = float(DH) ** -0.5

USES = {"A": {"S0": 1 + GROUPS + HEADS, "S1": 1 + GROUPS + HEADS, "T": 2 + UNITS, "O": 2 * 2 * GROUPS, "Y": 4},
        "B": {"S0": 1 + GROUPS + 2, "S1": 1 + GROUPS + 1, "T": 4, "O": 1 + TOK, "Y": 4}}

COPIES = ((0, 1), (2, 3), (0, 2), (1, 3), (0,))

C_ID, C_IOTA = 0, P
C_KEPT = C_HOT = C_IOTA + 8
C_FLIP = C_HOT + 512
C_SELECT = C_FLIP + P
C_ALL = C_SELECT + len(COPIES) * P


def constants():
    c = np.zeros((P, C_ALL), np.float32)
    c[:, C_ID:C_ID + P] = np.eye(P)
    row, col = np.arange(P)[:, None] % 32, np.arange(P)[None, :]
    for k, copies in enumerate(COPIES):
        hit = (row // 8 == col // 32) & (row % 8 == col % 8) & np.isin(col % 32 // 8, copies)
        c[:, C_SELECT + k * P:C_SELECT + (k + 1) * P] = hit
    c[:, C_IOTA:C_IOTA + 8] = np.arange(8)
    exact = BUCKETS // 2
    for x in range(2 * SEQ - 1):
        n = max(SEQ - 1 - x, 0)
        if n < exact:
            b = n
        else:
            ratio = np.log(np.float32(n) / np.float32(exact)) / np.float32(np.log(BUCKETS / exact))
            b = min(exact + int(ratio * np.float32(BUCKETS - exact)), BUCKETS - 1)
        c[b, C_HOT + x] = 1.0
    c[:, C_FLIP:C_FLIP + P] = np.eye(P)[::-1]
    return c


class Pass:

    def __init__(self, kind, i):
        self.kind, self.i = kind, i
        self.g = i if kind == "A" else i + PASSES
        self.first = isinstance(i, int) and i == 0

    def count(self, per, n):
        before = 0 if self.kind == "A" else PASSES * per["A"]
        return self.i * per[self.kind] + (CREDIT + before + n)


def segments(n):
    out = []
    for e in range(EXPERTS):
        lo, hi = max(e * INNER - n * P, 0), min((e + 1) * INNER - n * P, P)
        if lo < hi:
            out.append((e, lo, hi))
    return out


def weight_loads():
    out = []
    for n in range(SHARED_TILES, FT):
        parts = segments(n)
        if len(parts) == 1:
            parts = [(parts[0][0], 0, P)]
        if out and out[-1][0] == parts:
            out[-1][1].append(n)
        else:
            out.append((parts, [n]))
    return out


LOADS = weight_loads()
LOAD_OF = {n: k for k, (_, tiles) in enumerate(LOADS) for n in tiles}


def same(n):
    return {"A": n, "B": n}


NORM_PARTS, ROUTE_PARTS = 4 + NEWTON, 5

WORK = {
    "keep": {"pool": 1.8}, "load": {"sync": 3.0}, "norm1": {"dve": 0.6}, "turn1": {"pe": 0.5, "act": 0.5},
    "qk": {"pe": 0.85, "act": 0.6, "dve": 1.1}, "spread": {"pe": 0.43, "act": 0.5}, "v": {"pe": 0.9, "dve": 0.6},
    "scores": {"pe": 0.25, "dve": 0.75, "act": 0.8}, "probs": {"pe": 0.45, "act": 0.5},
    "mix": {"pe": 1.0, "dve": 0.35}, "context": {"pe": 0.25, "dve": 0.7},
    "bscores": {"pe": 0.5, "dve": 1.4, "act": 0.5}, "bprobs": {"dve": 0.6}, "bmix": {"pe": 0.35, "dve": 0.6},
    "bturn": {"pe": 0.5, "act": 0.5}, "bout": {"pe": 0.9, "dve": 0.6}, "norm2": {"dve": 0.6},
    "turn2": {"pe": 0.5, "act": 0.5}, "begin": {"dve": 1.0, "pe": 0.1, "pool": 1.8},
    "logits": {"pe": 1.6, "dve": 0.3}, "route": {"dve": 0.6, "act": 0.1},
    "wturn": {"pe": 0.5, "dve": 0.6, "act": 0.1, "sync": 4.0}, "gate": {"pe": 0.65, "act": 0.5, "dve": 0.6},
    "up": {"pe": 0.65, "dve": 0.6}, "weigh": {"pool": 1.25}, "cut": {"act": 0.55, "pool": 1.25, "dve": 0.6},
    "down": {"pe": 0.65}, "sum": {"act": 0.5}, "end": {"pe": 0.5, "dve": 0.6, "act": 0.1},
}
FLOW = ("pe", "act", "dve", "pool", "sync")
RULES = {
    "A": {"first": "longest chain", "experts": 1.0, "hand over": 0.3, "work": {
        ("dve", "context"): 0.88, ("dve", "up"): 0.66, ("pe", "begin"): 0.12, ("pe", "qk"): 1.06,
        ("sync", "load"): 3.75, ("sync", "wturn"): 3.6}},
    "B": {"first": "further behind", "experts": 0.97, "hand over": 0.15, "work": {
        ("act", "bturn"): 0.8, ("act", "gate"): 0.62, ("act", "spread"): 0.5, ("act", "turn1"): 0.62,
        ("act", "turn2"): 0.8, ("act", "wturn"): 0.12, ("pool", "cut"): 1.12}},
    "attention": {"first": "longest chain", "experts": 1.0, "hand over": 0.1, "work": {}},
    "experts": {"first": "longest chain", "experts": 0.752, "hand over": 0.05, "work": {
        ("act", "turn2"): 0.8, ("dve", "gate"): 0.48, ("dve", "up"): 0.32, ("pe", "turn2"): 0.27, ("pe", "up"): 0.39,
        ("pool", "begin"): 1.44}},
}
OWN = 0.06


def needs_attention(kind, eng, step, n):
    if step == "keep":
        return [("pool", "begin", 0)]
    if step == "load":
        return [("pool", "keep", 0)]
    if step == "norm1":
        return [("dve", "norm1", n - 1) if n else ("sync", "load", 0)] \
            + ([("pe", "turn1" if kind == "A" else "bturn", 0)] if n == NORM_PARTS - 1 else [])
    if step == "turn1":
        return [] if eng == "pe" else [("pe", "turn1", 0)]
    if step == "qk":
        return [{"pe": ("act", "turn1", 0), "act": ("pe", "qk", n), "dve": ("act", "qk", n)}[eng]]
    if step == "spread":
        return [("dve", "qk", n % 2), ("act", "spread", n - 2) if n > 1 else ("act", "qk", n)] if eng == "pe" \
            else [("pe", "spread", n)]
    if step == "v":
        return [("act", "turn1", 0)] if eng == "pe" else [("pe", "v", 0)]
    if step == "scores":
        if eng == "pe":
            return [("dve", "scores", n - 2)] if n > 1 else [("act", "spread", n) for n in range(2 * GROUPS)]
        if eng == "dve":
            return [("pe", "scores", n)] + ([("pe", "probs", n - Z_RING)] if n >= Z_RING else [])
        return [("dve", "scores", n)]
    if step == "probs":
        if eng == "pe":
            return [("act", "scores", n), ("act", "probs", n - 1) if n else ("dve", "v", 0)]
        return [("pe", "probs", n)] + ([("pe", "mix", (n - PT_RING) // 4)] if n >= PT_RING else [])
    if step == "mix":
        if eng == "pe":
            return [("act", "probs", 4 * n + 3)] + ([("dve", "context", n - 1)] if n else [])
        return [("pe", "mix", n)]
    if step == "context":
        return [("dve", "mix", n)] if eng == "pe" else [("pe", "context", n), ("pool", "keep", 0)]
    if step == "bscores":
        if eng == "pe":
            return [("act", "spread", n) for n in range(2 * GROUPS)] + [("dve", "v", 0)]
        return [("pe", "bscores", n)] if eng == "dve" else [("dve", "bscores", n)]
    if step == "bprobs":
        return [("act", "bscores", 4 * n + 3)]
    if step == "bmix":
        if eng == "pe":
            return [("dve", "bprobs", 3)] + ([("dve", "bmix", n // 4 * 4 - 1)] if n > 3 else [])
        return [("pe", "bmix", n)]
    if step == "bturn":
        return [("dve", "bmix", 4 * TOK - 1)] if eng == "pe" else [("pe", "bturn", 0)]
    if step == "bout":
        return [("act", "bturn", 0)] if eng == "pe" else [("pe", "bout", 0), ("pool", "keep", 0)]
    if step == "norm2":
        return [("dve", "norm2", n - 1) if n else ("dve", "context", 2 * GROUPS - 1) if kind == "A"
                else ("dve", "bout", 0)] + ([("pe", "turn2", 0)] if n == NORM_PARTS - 1 else [])


def needs_experts(low, eng, step, n):
    if step == "turn2":
        return [] if eng == "pe" else [("pe", "turn2", 0)]
    if step == "logits":
        return [("act", "turn2", 0)] if eng == "pe" else [("pe", "logits", 0)]
    if step == "route":
        if eng == "act":
            return [("dve", "route", 1)]
        return [("dve", "route", n - 1) if n else ("dve", "logits", 0)] + ([("act", "route", 1)] if n == 3 else [])
    if step == "wturn":
        return [{"pe": ("dve", "route", ROUTE_PARTS - 1), "dve": ("pe", "wturn", 0), "act": ("dve", "wturn", 0),
                 "sync": ("act", "wturn", 0)}[eng]]
    if step == "begin":
        return {"pe": [("dve", "begin", 0)], "dve": [("act", "turn2", 0)], "pool": []}[eng]
    if step == "gate":
        if eng == "pe":
            return [("dve", "up", n - 2)] if n > 1 else [("pe", "begin", 0)]
        if eng == "act":
            return [("pe", "gate", n)] + ([("dve", "up", n - 2)] if n > 1 else [])
        return [("act", "gate", n)]
    if step == "up":
        if eng == "pe":
            return [("dve", "gate", n - 1)] if n else [("pe", "begin", 0)]
        return [("pe", "up", n), ("dve", "gate", n)] + ([(low, "cut", n - H_RING)] if n >= H_RING else [])
    if step == "weigh":
        return [("dve", "up", n), ("sync", "wturn", 0)]
    if step == "cut":
        if eng == "act":
            return [("pool", "weigh", n) if n >= SHARED_TILES else ("dve", "up", n)] \
                + ([("pe", "down", n - CUT_RING)] if n >= CUT_RING else [])
        return [("act", "cut", n)]
    if step == "down":
        return [(low, "cut", n)] + ([] if n else [("dve", "wturn", 0)])
    if step == "sum":
        return [("pe", "down", FT - 1)]
    if step == "end":
        if eng == "pe":
            return [("act", "sum", 0)]
        return [("pe", "end", 0)] if eng == "dve" else [("dve", "end", 0)]


NORM1 = [("norm1", n) for n in range(NORM_PARTS)]


def steps_attention(kind, ahead):
    out = [("keep", 0), ("turn1", 0)] + ([("load", 0)] + NORM1 if ahead else [])
    out += [("qk", 0), ("qk", 1), ("v", 0)] + [("spread", n) for n in range(2 * GROUPS)]
    if kind == "A":
        for u in range(UNITS):
            out += [("scores", u), ("probs", u)]
            if u % 4 == 3:
                out += [("mix", u // 4), ("context", u // 4)]
    else:
        out += [("bscores", n) for n in range(4 * TOK)] + [("bprobs", r) for r in range(4)]
        out += [("bmix", n) for n in range(4 * TOK)] + [("bturn", 0), ("bout", 0)]
    return out + [("norm2", n) for n in range(NORM_PARTS)]


def steps_experts():
    out = [("turn2", 0), ("begin", 0), ("logits", 0)]
    out += [("route", n) for n in range(ROUTE_PARTS)] + [("wturn", 0)]
    for i in range(FT):
        out += [("gate", i), ("up", i), ("weigh", i), ("cut", i), ("down", i)]
    return out + [("sum", 0), ("end", 0)]


def low_engine(with_attention):
    return "pool" if with_attention else "dve"


def takes_part(kind, eng, step, n, low):
    if step == "cut":
        return eng in ("act", low)
    if eng not in WORK[step]:
        return False
    if eng == "act" and step == "route":
        return n == 1
    if step == "weigh":
        return n >= SHARED_TILES
    if eng != "pe" and step in ("bscores", "bmix"):
        return n % 4 == 3
    return True


def order(kind, attention, experts):
    low = low_engine(bool(attention))
    left = {e: [] for e in FLOW}
    needs, tail = {}, {}
    for is_expert, steps in ((True, experts), (False, attention)):
        for e in FLOW:
            mine = [s for s in steps if takes_part(kind, e, *s, low)]
            left[e].append(mine)
            for s in mine:
                w = needs_experts(low, e, *s) if is_expert else needs_attention(kind, e, *s)
                needs[(e,) + s] = w
    needs = {t: [x for x in w if x in needs] for t, w in needs.items()}
    users = {t: [] for t in needs}
    total = {e: [len(l) or 1 for l in left[e]] for e in FLOW}
    for t, ws in needs.items():
        for w in ws:
            users[w].append(t)

    def chain(t):
        if t not in tail:
            tail[t] = work(t) + max([hand_over + chain(u) for u in users[t]], default=0.0)
        return tail[t]

    rule = RULES[kind if attention and experts else "attention" if attention else "experts"]
    hand_over = rule["hand over"]

    def work(t):
        return rule["work"].get((t[0], t[1]), WORK[t[1]][t[0]])

    done, free, out = {}, {e: 0.0 for e in FLOW}, {e: [] for e in FLOW}
    while any(any(l) for l in left.values()):
        best = None
        for e in FLOW:
            for k, steps in enumerate(left[e]):
                seen = set()
                for s in steps:
                    t = (e,) + s
                    if s[0] not in seen and all(w in done for w in needs[t]):
                        start = max([free[e]] + [done[w] + (hand_over if w[0] != e else OWN) for w in needs[t]])
                        if rule["first"] == "longest chain":
                            urgency = chain(t)
                        else:
                            urgency = len(steps) / total[e][k]
                        key = (start, -urgency * (rule["experts"] if k == 0 else 1.0))
                        if best is None or key < best[0]:
                            best = (key, k, t, start)
                    seen.add(s[0])
        _, k, t, start = best
        e, s = t[0], t[1:]
        left[e][k].remove(s)
        free[e] = done[t] = start + work(t)
        out[e].append((k == 0,) + s)
    return out


FIRST = order("A", NORM1, [])
ALONE = {k: order(k, steps_attention(k, True), []) for k in "AB"}
BESIDE = {k: order(k, steps_attention(k, True), steps_experts()) for k in "AB"}
BESIDE_LAST = {k: order(k, steps_attention(k, False), steps_experts()) for k in "AB"}
EXPERTS_ALONE = order("A", [], steps_experts())


def run_passes(engine, name, attention, experts, before=lambda: None, after=lambda: None):
    def run(steps, this, following, ahead):
        before()
        for is_expert, step, n in steps[name]:
            if is_expert:
                experts(this, step, n)
            elif step in ("load", "norm1"):
                attention(ahead, step, n)
            else:
                attention(following, step, n)
        after()

    for kind in "AB":
        run(FIRST, None, None, Pass(kind, 0))
        run(ALONE[kind], None, Pass(kind, 0), Pass(kind, 1))
        with engine.Fori(0, PASSES - 2) as i:
            run(BESIDE[kind], Pass(kind, i), Pass(kind, i + 1), Pass(kind, i + 2))
        run(BESIDE_LAST[kind], Pass(kind, PASSES - 2), Pass(kind, PASSES - 1), None)
        run(EXPERTS_ALONE, Pass(kind, PASSES - 1), None, None)


def spread(ap, axis, n):
    ap = ap.unsqueeze(axis)
    shape = list(ap.shape)
    shape[axis] = n
    return ap.broadcast_to(shape)


def program(nc, x, w_qk, b_qk, w_vvo, b_rows, rel, wg, wu, wd, wr, const, out):
    def sb(name, shape, dt=F32):
        return nc.alloc_sbuf_tensor(name, shape, dt)

    cst = sb("cst", [P, C_KEPT])
    ident = cst[:, C_ID:C_ID + P]
    select = sb("select", [P, len(COPIES), P], F32R)
    proj = sb("proj", [P, 2, 2, P])
    proj_vo = sb("proj_vo", [P, 3, P])
    bcol = sb("bcol", [P, 2, 2])
    bc = sb("bc", [P, 3 * P + 8])
    router = sb("router", [P, 8])
    w_hi = [sb(f"w{n}_hi", [P, EXPERTS * INNER], F32R) for n in "gu"]
    w_lo = [sb(f"w{n}_lo", [P, EXPERTS * INNER], F32R) for n in "gu"]
    wd_hi = sb("wd_hi", [P, FT * P], F32R)
    wd_lo = sb("wd_lo", [P, FT * P], F32R)
    big = sb("big", [P, HEADS * 3 * P])
    bias_a = big[:, :].rearrange("p (h y) -> p h y", h=HEADS)
    qb = big[:, 0:GROUPS * CHUNK].rearrange("p (g t) -> p g t", g=GROUPS)
    kb = big[:, GROUPS * CHUNK:2 * GROUPS * CHUNK].rearrange("p (g t) -> p g t", g=GROUPS)

    xin = sb("xin", [P, TOK, D])
    xn = sb("xn", [P, TOK, D])
    xnT = sb("xnT", [P, CHUNK])
    xn2 = sb("xn2", [P, TOK, D])
    stats = sb("stats", [P, 2, TOK, 6])
    moments = sb("moments", [P, 2, TOK, 2])
    rs = sb("rs", [P, 2, 4, TOK])
    qk_hi = sb("qk_hi", [P, 2, CHUNK], F32R)
    qk_lo = sb("qk_lo", [P, 2, CHUNK], F32R)
    qk = sb("qk", [P, 2, CHUNK])
    qx = sb("qx", [P, GROUPS, CHUNK], F32R)
    kx = sb("kx", [P, GROUPS, CHUNK], F32R)
    vx = sb("vx", [P, TOK, HEADS * VW + 32 - VW])
    z = sb("z", [P, Z_RING, 2 * SEQ])
    nm = sb("nm", [P, NM_RING, 2])
    probT = sb("probT", [P, PT_RING, 2 * SEQ])
    oT = sb("oT", [P, 2, SEQ])
    rec = sb("rec", [P, HEADS])
    ctxt = sb("ctxt", [P, 2, 4, DH])
    h1 = sb("h1", [P, TOK, D])
    xf = sb("xf", [P, CHUNK])
    lg = sb("lg", [P, TOK, 8])
    top = sb("top", [P, TOK, 8])
    at = sb("at", [P, TOK, 8], U32)
    atf = sb("atf", [P, TOK, 8])
    gap = sb("gap", [P, TOK])
    e2 = sb("e2", [P, TOK])
    share = sb("share", [P, 3, TOK])
    wtok = sb("wtok", [P, 3, TOK, 8])
    wts = sb("wts", [8, CHUNK])
    maxb = sb("maxb", [P, 4, HEADS])
    ctxb = xn
    ctxT = xnT
    B_BANKS = (("S0", GROUPS + 1), ("S1", GROUPS + 1), ("T", 2), ("O", 0))

    xh = sb("xh", [P, CHUNK], F32R)
    xl = sb("xl", [P, CHUNK], F32R)
    hid_hi = sb("hid_hi", [P, CUT_RING, CHUNK], F32R)
    hid_lo = sb("hid_lo", [P, CUT_RING, CHUNK], F32R)
    work = sb("work", [P, 9 * CHUNK])
    stage = work[:, 0:PIECES * STAGE].rearrange("p (s c) -> p s c", s=PIECES)
    slot = work[:, :].rearrange("p (s c) -> p s c", c=CHUNK)
    th = slot[:, 0:2, :]
    total = th[:, 0, :]
    hid = slot[:, 2:2 + H_RING, :]
    weight = slot[:, 5:5 + WB_RING, :]
    h1F = slot[:, 7, :].rearrange("p (t d) -> p t d", t=TOK)
    xo = slot[:, 8, :].rearrange("p (t d) -> p t d", t=TOK)

    trev = z[0:HEADS, 2, :]
    relb = z[0:BUCKETS, 3, 0:HEADS]
    hot = stage[0:BUCKETS, 2, 0:512]
    flip = stage[:, 2, 512:512 + P]
    select_raw = stage[:, 2, 512 + P:512 + P + len(COPIES) * P].rearrange("p (k c) -> p k c", c=P)

    BANKS = ("S0", "S1", "T", "O", "E0", "E1", "E2", "Y")
    bank = {n: nc.alloc_psum_tensor(f"bank_{n}", [P, 512], F32) for n in BANKS}

    trev_dram = nc.dram_tensor("trev_dram", [HEADS, 512], F32).ap()
    x2 = nc.dram_tensor("x2", [BATCH * SEQ, D], F32).ap()
    wts_dram = nc.dram_tensor("wts_dram", [2 * PASSES, 8, CHUNK], F32).ap()

    sem = nc.alloc_semaphore
    setup_landed, weights_landed = sem("setup_landed"), sem("weights_landed")
    trev_stored, bias_landed = sem("trev_stored"), sem("bias_landed")
    flipped, bias_ready = sem("flipped"), sem("bias_ready")
    piece_landed = [sem(f"piece_landed_{k}") for k in range(2 * PIECES)]
    x_landed, stored = sem("x_landed"), sem("stored")
    setup_dve, setup_pe = sem("setup_dve"), sem("setup_pe")
    halved, high_cut, pieces_cut = sem("halved"), sem("high_cut"), sem("pieces_cut")
    filled = {n: sem(f"filled_{n}") for n in ("S0", "S1", "T", "O", "Y")}
    emptied = {n: sem(f"emptied_{n}") for n in ("S0", "S1", "T", "O", "Y")}
    normed1, kept, qk_cut, exp_done = sem("normed1"), sem("kept"), sem("qk_cut"), sem("exp_done")
    turned, h1_part, normed2 = sem("turned"), sem("h1_part"), sem("normed2")
    gap_ready, e2_ready, routed, vstep = sem("gap_ready"), sem("e2_ready"), sem("routed"), sem("vstep")
    wts_stored, weight_landed = sem("wts_stored"), [sem(f"weight_landed_{k}") for k in range(WB_RING)]
    xh_ready, xl_ready, h1F_ready = sem("xh_ready"), sem("xl_ready"), sem("h1F_ready")
    gate_done, up_done = sem("gate_done"), sem("up_done")
    th_ready, a_ready, h_ready = sem("th_ready"), sem("a_ready"), sem("h_ready")
    hh_ready, hl_ready, down_done = sem("hh_ready"), sem("hl_ready"), sem("down_done")
    weighed, summed = sem("weighed"), sem("summed")

    PASS_SCORES = {"A": UNITS, "B": TOK}

    def use(p, name, n):
        return p.count({k: USES[k][name] for k in "AB"}, n + 1)

    def landed(p):
        return (p.i + 1) * 16 if p.kind == "A" else (p.i + 1) * 64 + 16 * PASSES

    passed = {}

    def alone(eng):
        if eng not in passed:
            passed[eng] = sem(f"passed_{len(passed)}")
        eng.sem_inc(passed[eng], 1)

    def last_use(p, name):
        return USES[p.kind][name] - 1

    def weighed_count(p, n):
        return p.count(same(FT - SHARED_TILES), n - SHARED_TILES + 1)

    def weights_in(p, k):
        per_pass, upto = (sum(len(parts) for parts, _ in LOADS[k % WB_RING:end:WB_RING]) for end in (len(LOADS), k + 1))
        return 16 * (p.g * per_pass + upto)

    def product_bank(m):
        return bank[("E0", "E1", "E2")[m % 3]]

    def positions(rows, i, j):
        v = rows.rearrange("(l c t j) d -> j l c t d", l=BATCH, c=PASSES, t=TOK)[j]
        return v[:, bass.ds(i, 1), :, :].rearrange("l a t d -> l (a t) d")

    def turned_out(eng, copy, p, n):
        eng.wait_ge(filled["T"], use(p, "T", 2 + n))
        eng.wait_ge(filled["O"], use(p, "O", 2 * ((n - PT_RING) // 4)))
        copy(probT[:, n % PT_RING, :], bank["T"][:, :]).then_inc(emptied["T"], 1)

    def of_pass(p):
        return wts_dram[bass.ds(p.g, 1), :, :].rearrange("a e t -> (a e) t")

    def cut_low(eng, p, n):
        eng.wait_ge(hh_ready, p.count(same(FT), n + 1))
        eng.wait_ge(down_done, p.count(same(FT), n + 1 - CUT_RING))
        eng.tensor_tensor(hid_lo[:, n % CUT_RING, :], hid[:, n % H_RING, :], hid_hi[:, n % CUT_RING, :].bitcast(F32),
                          ALU.subtract).then_inc(hl_ready, 1)

    with nc.Block() as block:
        @block.sync
        def _(sp):
            sp.sem_inc(stored, 16)
            sp.dma_start(relb, rel).then_inc(setup_landed, 16)
            sp.dma_start(hot, const[0:BUCKETS, C_HOT:C_HOT + 512]).then_inc(setup_landed, 16)
            sp.dma_start(cst[:, :], const[:, 0:C_KEPT]).then_inc(setup_landed, 16)
            sp.dma_start(flip, const[:, C_FLIP:C_SELECT]).then_inc(setup_landed, 16)
            sp.dma_start(select_raw, const[:, C_SELECT:C_ALL].rearrange("p (k c) -> p k c", c=P)
                         ).then_inc(setup_landed, 16)

            def load(p):
                sp.wait_ge(normed1, p.count(same(1), 0))
                sp.wait_ge(kept, p.count(same(1), 0))
                if p.kind == "A":
                    src = x[bass.ds(p.i * CHUNK, CHUNK), :].rearrange("(t p) d -> p t d", p=P)
                    sp.dma_start(xin[:, :, :], src).then_inc(x_landed, 16)
                    return
                if p.first:
                    sp.wait_ge(stored, 16 * (PASSES + 1))
                for j in range(4):
                    sp.dma_start(xin[32 * j:32 * j + 32, :, :], positions(x2, p.i, j)).then_inc(x_landed, 16)

            def spread_weights(p):
                sp.wait_ge(wts_stored, 16 * p.g + 16)
                for k, (parts, _) in enumerate(LOADS):
                    last = LOADS[k - WB_RING][1][-1] if k >= WB_RING else SHARED_TILES - 1
                    sp.wait_ge(weighed, weighed_count(p, last))
                    for e, lo, hi in parts:
                        r = (e - 1) % EXPERTS
                        row = of_pass(p)[r:r + 1, :]
                        sp.dma_start(weight[lo:hi, k % WB_RING, :],
                                     bass.AP(row.tensor, row.offset, [[0, hi - lo], [1, CHUNK]])
                                     ).then_inc(weight_landed[k % WB_RING], 16)

            load(Pass("A", 0))
            sp.dma_start(proj[:, :, :, :], w_qk).then_inc(weights_landed, 16)
            sp.dma_start(bcol[:, :, :], b_qk).then_inc(weights_landed, 16)
            sp.dma_start(proj_vo[:, :, :], w_vvo).then_inc(weights_landed, 16)
            width = 3 * P + 7
            sp.dma_start(bc[:, 0:width], bass.AP(b_rows.tensor, b_rows.offset, [[0, P], [1, width]])
                         ).then_inc(weights_landed, 16)
            sp.dma_start(router[:, 0:7], wr).then_inc(weights_landed, 16)
            sp.wait_ge(setup_dve, 5)
            sp.dma_start(trev_dram, trev).then_inc(trev_stored, 16)
            sp.wait_ge(trev_stored, 16)
            skewed = bass.AP(trev_dram.tensor, trev_dram.offset, [[1, P], [512, HEADS], [1, 3 * P]])
            sp.dma_start(bias_a, skewed).then_inc(bias_landed, 16)
            load(Pass("A", 1))
            for k in range(2 * PIECES):
                if k == 2:
                    sp.wait_ge(flipped, HEADS)
                    sp.wait_ge(setup_dve, 8)
                if k >= PIECES:
                    sp.wait_ge(pieces_cut, k - PIECES + 1)
                dst = stage[:, k % PIECES, :]
                if k < 4:
                    src = (wg, wu)[k // 2][:, (k % 2) * STAGE:(k % 2 + 1) * STAGE]
                else:
                    src = wd[(k % 2) * STAGE:(k % 2 + 1) * STAGE, :].rearrange("(t p) h -> p t h", p=P)
                    dst = dst.rearrange("p (t h) -> p t h", h=P)
                sp.dma_start(dst, src).then_inc(piece_landed[k], 16)
            sp.wait_ge(pieces_cut, 2 * PIECES)
            for kind in "AB":
                if kind == "B":
                    load(Pass("B", 0))
                    load(Pass("B", 1))
                with sp.Fori(0, PASSES - 2) as i:
                    load(Pass(kind, i + 2))
                    spread_weights(Pass(kind, i))
                for i in range(PASSES - 2, PASSES):
                    spread_weights(Pass(kind, i))
            sp.wait_ge(wts_stored, 16 * 2 * PASSES)
            sp.wait_ge(stored, 16 * (1 + PASSES + 4 * PASSES))

        @block.gpsimd
        def _(pool):
            for s in (kept, hl_ready, h1F_ready, weighed):
                pool.sem_inc(s, CREDIT)

            def keep(p):
                pool.wait_ge(x_landed, landed(p))
                pool.wait_ge(normed2, p.count(same(1), 0))
                pool.wait_ge(h1F_ready, p.count(same(1), 0))
                alone(pool)
                if p.kind == "A":
                    pool.tensor_copy(h1[:, :, :], xin[:, :, :]).then_inc(kept, 1)
                else:
                    pool.tensor_tensor(h1[:, :, :], xin[:, :, :], spread(bc[:, 2 * P:3 * P], 1, TOK),
                                       ALU.add).then_inc(kept, 1)

            def attention(p, step, n):
                if step == "keep":
                    keep(p)

            def experts(p, step, n):
                if step == "begin":
                    if p.kind == "A":
                        pool.wait_ge(h1_part, p.count({"A": 2 * GROUPS, "B": 0}, 2 * GROUPS))
                    else:
                        pool.wait_ge(emptied["S0"], use(p, "S0", last_use(p, "S0")))
                    pool.wait_ge(emptied["Y"], use(p, "Y", -1))
                    alone(pool)
                    pool.tensor_copy(h1F, h1[:, :, :]).then_inc(h1F_ready, 1)
                elif step == "weigh":
                    k = LOAD_OF[n]
                    pool.wait_ge(weight_landed[k % WB_RING], weights_in(p, k))
                    pool.wait_ge(h_ready, p.count(same(FT), n + 1))
                    h = hid[:, n % H_RING, :]
                    pool.tensor_tensor(h, h, weight[:, k % WB_RING, :], ALU.mult).then_inc(weighed, 1)
                elif step == "cut":
                    cut_low(pool, p, n)

            first = Pass("A", 0)
            keep(first)
            for k in range(2 * PIECES):
                pool.wait_ge(piece_landed[k], 16)
                raw, lo = stage[:, k % PIECES, :], (k % 2) * STAGE
                if k < 4:
                    hi_dst, lo_dst = w_hi[k // 2][:, lo:lo + STAGE], w_lo[k // 2][:, lo:lo + STAGE]
                else:
                    hi_dst, lo_dst = wd_hi[:, lo:lo + STAGE], wd_lo[:, lo:lo + STAGE]
                    pool.tensor_scalar(raw, raw, 0.5, None, ALU.mult).then_inc(halved, 1)
                    pool.wait_ge(halved, k - 3)
                pool.tensor_copy(hi_dst, raw).then_inc(high_cut, 1)
                pool.wait_ge(high_cut, k + 1)
                pool.tensor_tensor(lo_dst, raw, hi_dst.bitcast(F32), ALU.subtract).then_inc(pieces_cut, 1)
            pool.wait_ge(pieces_cut, 2 * PIECES)
            pool.wait_ge(weights_landed, 5 * 16)

            def attention_but_first(p, step, n):
                if p.kind == "B" or not p.first:
                    attention(p, step, n)

            run_passes(pool, "pool", attention_but_first, experts)

        @block.scalar
        def _(act):
            for s in (exp_done, th_ready, hh_ready, e2_ready, summed):
                act.sem_inc(s, CREDIT)

            def attention(p, step, n):
                if step == "scores" and n == 0 and p.first:
                    for h in range(HEADS):
                        act.wait_ge(flipped, h + 1)
                        act.activation(bias_a[:, h, :], bank[("E0", "E1", "E2", "Y")[h % 4]][:, 0:3 * P], ACT.Copy
                                       ).then_inc(bias_ready, 1)
                if step == "turn1":
                    act.wait_ge(filled["T"], use(p, "T", 0))
                    act.activation(xnT[:, :], bank["T"][:, :], ACT.Copy).then_inc(emptied["T"], 1)
                elif step == "qk":
                    s, half = f"S{n}", "AB".index(p.kind)
                    act.wait_ge(filled[s], use(p, s, 0))
                    act.activation(qk[:, n, :], bank[s][:, :], ACT.Identity, bias=bcol[:, half, n:n + 1],
                                   scale=1.0 if n else SCALE).then_inc(emptied[s], 1)
                elif step == "spread":
                    s, g, m = f"S{n % 2}", n // 2, n % 2
                    act.wait_ge(filled[s], use(p, s, 1 + g))
                    dst = (qx, kx) if p.kind == "A" else (qb, kb)
                    act.activation(dst[m][:, g, :], bank[s][:, :], ACT.Copy).then_inc(emptied[s], 1)
                elif step == "scores":
                    act.wait_ge(emptied[f"S{n % 2}"], use(p, f"S{n % 2}", 1 + GROUPS + n // 2))
                    for t in range(2):
                        zt = z[:, n % Z_RING, t * SEQ:(t + 1) * SEQ]
                        last = act.activation(zt, zt, ACT.Exp, bias=nm[:, n % NM_RING, t:t + 1], scale=-1.0)
                    last.then_inc(exp_done, 1)
                elif step == "probs":
                    turned_out(act, act.copy, p, n)
                elif step == "bscores":
                    n = n // 4
                    s, k = B_BANKS[n]
                    act.wait_ge(emptied[s], use(p, s, k))
                    act.activation(z[:, n, :], z[:, n, :], ACT.Exp).then_inc(exp_done, 1)
                elif step == "bturn":
                    act.wait_ge(filled["T"], use(p, "T", 3))
                    act.activation(ctxT[:, :], bank["T"][:, :], ACT.Copy).then_inc(emptied["T"], 1)

            def experts(p, step, n):
                if step == "turn2":
                    act.wait_ge(filled["Y"], use(p, "Y", 0))
                    act.wait_ge(xl_ready, p.count(same(1), 0))
                    act.activation(xf[:, :], bank["Y"][:, :], ACT.Copy).then_inc(emptied["Y"], 1)
                elif step == "route":
                    act.wait_ge(gap_ready, p.count(same(1), 1))
                    act.activation(e2[:, :], gap[:, :], ACT.Exp).then_inc(e2_ready, 1)
                elif step == "wturn":
                    act.wait_ge(emptied["Y"], use(p, "Y", 2))
                    act.dma_start(of_pass(p), wts[:, :]).then_inc(wts_stored, 16)
                elif step == "end":
                    act.wait_ge(emptied["Y"], use(p, "Y", 3))
                    if p.kind == "A":
                        dst = x2[bass.ds(p.i * CHUNK, CHUNK), :].rearrange("(t p) d -> p t d", p=P)
                        act.dma_start(dst, xo).then_inc(stored, 16)
                    else:
                        for j in range(4):
                            act.dma_start(positions(out, p.i, j), xo[32 * j:32 * j + 32, :, :]).then_inc(stored, 16)
                elif step == "gate":
                    if n == 0:
                        act.wait_ge(filled["Y"], use(p, "Y", -1))
                    act.wait_ge(gate_done, p.count(same(FT), n + 1))
                    act.wait_ge(h_ready, p.count(same(FT), n - 1))
                    act.activation(th[:, n % 2, :], product_bank(2 * n)[:, :], ACT.Tanh, scale=0.5).then_inc(th_ready, 1)
                elif step == "cut":
                    if n < SHARED_TILES:
                        act.wait_ge(h_ready, p.count(same(FT), n + 1))
                    else:
                        act.wait_ge(weighed, weighed_count(p, n))
                    act.wait_ge(down_done, p.count(same(FT), n + 1 - CUT_RING))
                    act.activation(hid_hi[:, n % CUT_RING, :], hid[:, n % H_RING, :], ACT.Copy).then_inc(hh_ready, 1)
                elif step == "sum":
                    act.wait_ge(down_done, p.count(same(FT), FT))
                    act.wait_ge(h_ready, p.count(same(FT), FT))
                    act.activation(total, bank["Y"][:, :], ACT.Copy).then_inc(summed, 1)

            def experts_after_cuts(p, step, n):
                if step == "begin" and p.kind == "A":
                    act.wait_ge(pieces_cut, 2 * PIECES)
                experts(p, step, n)

            act.wait_ge(setup_dve, 8)
            run_passes(act, "act", attention, experts_after_cuts)

        @block.vector
        def _(dve):
            for s in (emptied["S0"], emptied["S1"], emptied["T"], emptied["O"], emptied["Y"], normed1, qk_cut,
                      turned, h1_part, normed2, gap_ready, routed, xh_ready, xl_ready,
                      a_ready, h_ready):
                dve.sem_inc(s, CREDIT)
            dve.memset(bc[:, 3 * P + 7:3 * P + 8], -FAR).then_inc(setup_dve, 1)
            dve.memset(router[:, 7:8], 0.0).then_inc(setup_dve, 1)
            dve.memset(vx[:, :, :], 1.0).then_inc(setup_dve, 1)
            dve.memset(wtok[:, 2, :, 7:8], 1.0).then_inc(setup_dve, 1)
            dve.wait_ge(setup_pe, 1)
            dve.tensor_copy(trev, bank["O"][0:HEADS, :]).then_inc(setup_dve, 1)
            dve.wait_ge(weights_landed, 5 * 16)
            for half in range(2):
                dve.tensor_scalar(bcol[:, half, 0:1], bcol[:, half, 0:1], SCALE, None, ALU.mult).then_inc(setup_dve, 1)
            dve.wait_ge(setup_landed, 5 * 16)
            dve.tensor_copy(select[:, :, :], select_raw).then_inc(setup_dve, 1)

            steps = [0]

            def then(instruction):
                mark(instruction)
                settle()

            def mark(instruction):
                steps[0] += 1
                instruction.then_inc(vstep, 1)

            def settle():
                dve.wait_ge(vstep, steps[0])

            def normalise(p, rows, dst, k, done, n):
                v, y, a, b = (rs[:, k, m, :] for m in range(4))
                if n > 0:
                    settle()
                if n == 0:
                    for t in range(TOK):
                        last = dve.bn_stats(stats[:, k, t, :], rows[:, t, :])
                    mark(last)
                elif n == 1:
                    for t in range(TOK):
                        last = dve.bn_aggr(moments[:, k, t, :], stats[:, k, t, :])
                    mark(last)
                elif n == 2:
                    then(dve.tensor_scalar(v, moments[:, k, :, 1], EPS, None, ALU.add))
                    mark(dve.tensor_scalar(y.bitcast(I32), v.bitcast(I32), -0.5, MAGIC, ALU.mult, ALU.add))
                elif n < NORM_PARTS - 1:
                    then(dve.scalar_tensor_tensor(out=a, in0=y, scalar=-0.5, in1=y, op0=ALU.mult, op1=ALU.mult))
                    then(dve.tensor_tensor(b, a, v, ALU.mult))
                    mark(dve.scalar_tensor_tensor(out=y, in0=b, scalar=1.5, in1=y, op0=ALU.add, op1=ALU.mult))
                else:
                    for t in range(TOK):
                        last = dve.tensor_scalar(dst[:, t, :], rows[:, t, :], moments[:, k, t, 0:1], y[:, t:t + 1],
                                                 ALU.subtract, ALU.mult)
                    last.then_inc(done, 1)

            def count_afresh():
                steps[0] = 1
                dve.sem_clear(vstep)
                dve.sem_inc(vstep, 1)

            def route(p, n):
                s, first, second = (share[:, k, :] for k in range(3))
                settle()
                if n == 0:
                    for t in range(TOK):
                        last = dve.max(top[:, t, :], lg[:, t, :])
                    mark(last)
                elif n == 1:
                    for t in range(TOK):
                        last = dve.max_index(at[:, t, :], top[:, t, :], lg[:, t, :])
                    mark(last)
                    dve.tensor_tensor(gap[:, :], top[:, :, 1], top[:, :, 0], ALU.subtract).then_inc(gap_ready, 1)
                elif n == 2:
                    mark(dve.tensor_copy(atf[:, :, :], at[:, :, :]))
                elif n == 3:
                    dve.wait_ge(e2_ready, p.count(same(1), 1))
                    then(dve.tensor_scalar(s, e2[:, :], 1.0, None, ALU.add))
                    then(dve.reciprocal(first, s))
                    mark(dve.tensor_tensor(second, e2[:, :], first, ALU.mult))
                elif n == 4:
                    for t in range(TOK):
                        for k, w in enumerate((first, second)):
                            last = dve.tensor_scalar(wtok[:, k, t, :], cst[:, C_IOTA:C_IOTA + 8], atf[:, t, k:k + 1],
                                                     w[:, t:t + 1], ALU.is_equal, ALU.mult)
                    then(last)
                    dve.tensor_tensor(wtok[:, 2, :, 0:7], wtok[:, 0, :, 0:7], wtok[:, 1, :, 0:7], ALU.add).then_inc(routed, 1)

            def attention(p, step, n):
                if step == "norm1":
                    if n == 0:
                        dve.wait_ge(x_landed, landed(p))
                    if n == NORM_PARTS - 1 and not p.first:
                        back = USES[p.kind]["T"]
                        dve.wait_ge(filled["T"], use(p, "T", (0 if p.kind == "A" else 3) - back))
                    normalise(p, xin, xn, 0, normed1, n)
                elif step == "qk":
                    dve.wait_ge(emptied[f"S{n}"], use(p, f"S{n}", 0))
                    then(dve.tensor_copy(qk_hi[:, n, :], qk[:, n, :]))
                    dve.tensor_tensor(qk_lo[:, n, :], qk[:, n, :], qk_hi[:, n, :].bitcast(F32), ALU.subtract
                                      ).then_inc(qk_cut, 1)
                elif step == "v":
                    m = "AB".index(p.kind)
                    dve.wait_ge(filled["T"], use(p, "T", 1))
                    dst = vx[:, :, 0:HEADS * VW].rearrange("p t (h c) -> p t h c", c=VW)[:, :, :, 0:DH]
                    src = bank["T"][:, :].rearrange("p (t h d) -> p t h d", t=TOK, d=DH)
                    b = spread(bc[:, m * P:(m + 1) * P].rearrange("p (h d) -> p h d", d=DH), 1, TOK)
                    dve.tensor_tensor(dst, src, b, ALU.add).then_inc(emptied["T"], 1)
                elif step == "scores":
                    s, h = f"S{n % 2}", n % HEADS
                    if n == 0:
                        dve.wait_ge(bias_ready, HEADS)
                    dve.wait_ge(filled[s], use(p, s, 1 + GROUPS + n // 2))
                    dve.wait_ge(filled["T"], use(p, "T", 2 + n - Z_RING))
                    alone(dve)
                    for t in range(2):
                        last = dve.tensor_tensor_reduce(
                            z[:, n % Z_RING, t * SEQ:(t + 1) * SEQ], bank[s][:, t * SEQ:(t + 1) * SEQ],
                            bias_a[:, h, P - P * t:P - P * t + SEQ], -1.0, FAR, ALU.add, ALU.min,
                            nm[:, n % NM_RING, t:t + 1])
                    last.then_inc(emptied[s], 1)
                elif step == "mix":
                    dve.wait_ge(filled["O"], use(p, "O", 2 * n))
                    dve.tensor_copy(oT[:, n % 2, :], bank["O"][:, 0:SEQ]).then_inc(emptied["O"], 1)
                elif step == "context":
                    dve.wait_ge(filled["O"], use(p, "O", 2 * n + 1))
                    o = bank["O"][:, 0:SEQ].rearrange("p (t j c) -> p (t j) c", t=2, j=4)
                    c8 = ctxt[:, :, :, :].rearrange("p t j d -> p (t j) d")
                    then(dve.reciprocal(rec[:, 0:8], o[:, :, DH]))
                    dve.tensor_tensor(c8, o[:, :, 0:DH], spread(rec[:, 0:8], 2, DH), ALU.mult).then_inc(emptied["O"], 1)
                    dve.wait_ge(emptied["O"], use(p, "O", 2 * n + 1))
                    dve.wait_ge(kept, p.count(same(1), 1))
                    b, g = n // GROUPS, n % GROUPS
                    dst = h1[:, 2 * b:2 * b + 2, 32 * g:32 * g + 32]
                    dve.tensor_tensor(dst, dst, ctxt[:, :, :, :].rearrange("p t j d -> p t (j d)"), ALU.add
                                      ).then_inc(h1_part, 1)
                elif step == "bscores":
                    n = n // 4
                    s, k = B_BANKS[n]
                    dve.wait_ge(filled[s], use(p, s, k))
                    sc = bank[s][:, :].rearrange("p (h m) -> p h m", m=32)
                    then(dve.tensor_reduce(maxb[:, n, :], sc, AX.X, ALU.max))
                    dve.wait_ge(turned, p.count({"A": 0, "B": 4}, n - 3))
                    dve.tensor_tensor(z[:, n, :].rearrange("p (h m) -> p h m", m=32), sc,
                                      spread(maxb[:, n, :], 2, 32), ALU.subtract).then_inc(emptied[s], 1)
                elif step == "bprobs":
                    dve.wait_ge(exp_done, p.count(PASS_SCORES, n + 1))
                    dve.transpose(probT[:, n, :], z[:, n, :]).then_inc(turned, 1)
                elif step == "bmix":
                    n = n // 4
                    dve.wait_ge(filled["O"], use(p, "O", 1 + n))
                    o = bank["O"][:, 0:HEADS * VW].rearrange("p (h c) -> p h c", c=VW)
                    then(dve.reciprocal(rec[:, :], o[:, :, DH]))
                    dve.tensor_tensor(ctxb[:, n, :].rearrange("p (h d) -> p h d", d=DH), o[:, :, 0:DH],
                                      spread(rec[:, :], 2, DH), ALU.mult).then_inc(emptied["O"], 1)
                elif step == "bout":
                    dve.wait_ge(filled["S0"], use(p, "S0", last_use(p, "S0")))
                    dve.wait_ge(kept, p.count(same(1), 1))
                    o = bank["S0"][:, :].rearrange("p (t d) -> p t d", t=TOK)
                    dve.tensor_tensor(h1[:, :, :], h1[:, :, :], o, ALU.add).then_inc(emptied["S0"], 1)
                elif step == "norm2":
                    if n == 0 and p.kind == "A":
                        dve.wait_ge(h1_part, p.count({"A": 2 * GROUPS, "B": 0}, 2 * GROUPS))
                    elif n == 0:
                        dve.wait_ge(emptied["S0"], use(p, "S0", last_use(p, "S0")))
                    if n == NORM_PARTS - 1:
                        dve.wait_ge(filled["Y"], use(p, "Y", -4))
                    normalise(p, h1, xn2, 1, normed2, n)

            def experts(p, step, n):
                if step == "logits":
                    dve.wait_ge(filled["Y"], use(p, "Y", 1))
                    dve.tensor_tensor(lg[:, :, :], bank["Y"][:, 0:8 * TOK].rearrange("p (t e) -> p t e", t=TOK),
                                      spread(bc[:, 3 * P:3 * P + 8], 1, TOK), ALU.add).then_inc(emptied["Y"], 1)
                    dve.wait_ge(emptied["Y"], use(p, "Y", 1))
                    alone(dve)
                elif step == "route":
                    route(p, n)
                elif step == "wturn":
                    dve.wait_ge(filled["Y"], use(p, "Y", 2))
                    if not (p.kind == "A" and p.first):
                        dve.wait_ge(wts_stored, 16 * p.g)
                    dve.tensor_copy(wts[:, :], bank["Y"][0:8, :]).then_inc(emptied["Y"], 1)
                elif step == "begin":
                    if p.kind == "A":
                        dve.wait_ge(pieces_cut, 2 * PIECES)
                    dve.wait_ge(filled["Y"], use(p, "Y", -1))
                    dve.wait_ge(emptied["Y"], use(p, "Y", 0))
                    dve.tensor_copy(xh[:, :], xf[:, :]).then_inc(xh_ready, 1)
                    dve.wait_ge(xh_ready, p.count(same(1), 1))
                    dve.tensor_tensor(xl[:, :], xf[:, :], xh[:, :].bitcast(F32), ALU.subtract).then_inc(xl_ready, 1)
                elif step == "gate":
                    dve.wait_ge(th_ready, p.count(same(FT), n + 1))
                    a = th[:, n % 2, :]
                    dve.scalar_tensor_tensor(out=a, in0=a, scalar=1.0, in1=product_bank(2 * n)[:, :], op0=ALU.add,
                                             op1=ALU.mult).then_inc(a_ready, 1)
                elif step == "up":
                    dve.wait_ge(a_ready, p.count(same(FT), n + 1))
                    dve.wait_ge(up_done, p.count(same(FT), n + 1))
                    dve.wait_ge(hl_ready, p.count(same(FT), n + 1 - H_RING))
                    dve.tensor_tensor(hid[:, n % H_RING, :], th[:, n % 2, :], product_bank(2 * n + 1)[:, :], ALU.mult
                                      ).then_inc(h_ready, 1)
                elif step == "cut":
                    cut_low(dve, p, n)
                elif step == "end":
                    dve.wait_ge(filled["Y"], use(p, "Y", 3))
                    dve.wait_ge(h1F_ready, p.count(same(1), 1))
                    dve.wait_ge(stored, p.i * 16 + 16 if p.kind == "A" else p.i * 64 + 16 * (PASSES + 1))
                    dve.tensor_tensor(xo, bank["Y"][:, :].rearrange("p (t d) -> p t d", t=TOK), h1F, ALU.add
                                      ).then_inc(emptied["Y"], 1)

            run_passes(dve, "dve", attention, experts, count_afresh, settle)

        @block.tensor
        def _(pe):
            for s in list(filled.values()) + [gate_done, up_done, down_done]:
                pe.sem_inc(s, CREDIT)
            pe.wait_ge(setup_landed, 5 * 16)
            pe.matmul(bank["O"][0:HEADS, :], relb, hot, start=True, stop=True).then_inc(setup_pe, 1)
            pe.wait_ge(setup_dve, 8)
            pe.wait_ge(weights_landed, 5 * 16)

            def next_use(p, name, n):
                pe.wait_ge(emptied[name], use(p, name, n - 1))

            def turn_rows(p, rows, name, n):
                next_use(p, name, n)
                for t in range(TOK):
                    last = pe.transpose(bank[name][:, t * P:(t + 1) * P], rows[:, t, :], ident)
                last.then_inc(filled[name], 1)

            def flip_biases():
                pe.wait_ge(bias_landed, 16)
                for h in range(HEADS):
                    if h >= 4:
                        pe.wait_ge(bias_ready, h - 3)
                    pe.matmul(bank[("E0", "E1", "E2", "Y")[h % 4]][:, 0:3 * P], flip, bias_a[:, h, :], start=True,
                              stop=True).then_inc(flipped, 1)

            def attention(p, step, n):
                half = "AB".index(p.kind)
                if step == "scores" and n == 0 and p.first:
                    flip_biases()
                if step == "turn1":
                    pe.wait_ge(normed1, p.count(same(1), 1))
                    turn_rows(p, xn, "T", 0)
                elif step == "qk":
                    pe.wait_ge(emptied["T"], use(p, "T", 0))
                    next_use(p, f"S{n}", 0)
                    pe.matmul(bank[f"S{n}"][:, :], proj[:, half, n, :], xnT[:, :], start=True, stop=True
                              ).then_inc(filled[f"S{n}"], 1)
                elif step == "spread":
                    s, g, m = f"S{n % 2}", n // 2, n % 2
                    pe.wait_ge(qk_cut, p.count(same(2), m + 1))
                    next_use(p, s, 1 + g)
                    rows = slice(32 * g, 32 * g + 32)
                    hi, lo = (4, 4) if half else (2 * m, 2 * m + 1)
                    pe.matmul(bank[s][:, :], select[rows, hi, :], qk_hi[rows, m, :], start=True, stop=False)
                    pe.matmul(bank[s][:, :], select[rows, lo, :], qk_lo[rows, m, :], start=False, stop=True
                              ).then_inc(filled[s], 1)
                elif step == "v":
                    next_use(p, "T", 1)
                    for t in range(TOK):
                        last = pe.matmul(bank["T"][:, t * P:(t + 1) * P], xnT[:, t * P:(t + 1) * P],
                                         proj_vo[:, half, :], start=True, stop=True)
                    last.then_inc(filled["T"], 1)
                elif step == "scores":
                    s, b, h = f"S{n % 2}", n // HEADS, n % HEADS
                    rows, g = slice(32 * (h % 4), 32 * (h % 4) + 32), h // 4
                    if n == 0:
                        for k in range(2):
                            pe.wait_ge(emptied[f"S{k}"], use(p, f"S{k}", GROUPS))
                    next_use(p, s, 1 + GROUPS + n // 2)
                    for t in range(2):
                        lo = b * SEQ + t * P
                        last = pe.matmul(bank[s][:, t * SEQ:(t + 1) * SEQ], qx[rows, g, lo:lo + P],
                                         kx[rows, g, b * SEQ:(b + 1) * SEQ], start=True, stop=True)
                    last.then_inc(filled[s], 1)
                elif step == "probs":
                    pe.wait_ge(exp_done, p.count(PASS_SCORES, n + 1))
                    next_use(p, "T", 2 + n)
                    for k in range(2):
                        for t in range(2):
                            c = k * SEQ + t * P
                            last = pe.transpose(bank["T"][:, c:c + P],
                                                z[:, n % Z_RING, t * SEQ + k * P:t * SEQ + (k + 1) * P], ident)
                    last.then_inc(filled["T"], 1)
                elif step == "mix":
                    pe.wait_ge(emptied["T"], use(p, "T", 2 + 4 * n + 3))
                    next_use(p, "O", 2 * n)
                    b, g = n // GROUPS, n % GROUPS
                    for k in range(2):
                        for j in range(4):
                            u, c = 4 * n + j, (4 * g + j) * VW
                            last = pe.matmul(bank["O"][32 * j:32 * j + 32, 0:SEQ], vx[:, 2 * b + k, c:c + 32],
                                             probT[:, u % PT_RING, k * SEQ:(k + 1) * SEQ], start=(k == 0),
                                             stop=(k == 1), tile_position=(0, 32 * j))
                    last.then_inc(filled["O"], 1)
                elif step == "context":
                    next_use(p, "O", 2 * n + 1)
                    for t in range(2):
                        last = pe.transpose(bank["O"][:, t * P:(t + 1) * P], oT[:, n % 2, t * P:(t + 1) * P], ident)
                    last.then_inc(filled["O"], 1)
                elif step == "bscores":
                    r, t = n // TOK, n % TOK
                    s, use_s = B_BANKS[r]
                    if t == 0:
                        for k in range(2):
                            pe.wait_ge(emptied[f"S{k}"], use(p, f"S{k}", GROUPS))
                        next_use(p, s, use_s)
                        alone(pe)
                    rows = slice(32 * r, 32 * r + DH)
                    for g in range(GROUPS):
                        c = (t * GROUPS + g) * 32
                        for j in range(4):
                            lo = t * P + 32 * j
                            last = pe.matmul(bank[s][32 * j:32 * j + 32, c:c + 32], qb[rows, g, lo:lo + 32],
                                             kb[rows, g, lo:lo + 32], start=True, stop=True,
                                             tile_position=(32 * r, 32 * j))
                    if t == TOK - 1:
                        last.then_inc(filled[s], 1)
                elif step == "bmix":
                    t, g = n // GROUPS, n % GROUPS
                    if g == 0:
                        pe.wait_ge(turned, p.count({"A": 0, "B": 4}, 4))
                        next_use(p, "O", 1 + t)
                        alone(pe)
                    c = (t * GROUPS + g) * 32
                    for h in range(4 * g, 4 * g + 4):
                        for j in range(4):
                            r = slice(32 * j, 32 * j + 32)
                            last = pe.matmul(bank["O"][r, h * VW:(h + 1) * VW], probT[r, h % 4, c:c + 32],
                                             vx[r, t, h * VW:(h + 1) * VW], start=True, stop=True,
                                             tile_position=(32 * j, 32 * j))
                    if g == GROUPS - 1:
                        last.then_inc(filled["O"], 1)
                elif step == "bturn":
                    pe.wait_ge(emptied["O"], use(p, "O", TOK))
                    turn_rows(p, ctxb, "T", 3)
                elif step == "bout":
                    pe.wait_ge(emptied["T"], use(p, "T", 3))
                    next_use(p, "S0", last_use(p, "S0"))
                    for t in range(TOK):
                        last = pe.matmul(bank["S0"][:, t * P:(t + 1) * P], ctxT[:, t * P:(t + 1) * P], proj_vo[:, 2, :],
                                         start=True, stop=True)
                    last.then_inc(filled["S0"], 1)

            def product(dst, high_w, low_w, high_x, low_x, start=True, stop=True):
                pe.matmul(dst, high_w, high_x, start=start, stop=False)
                pe.matmul(dst, high_w, low_x, start=False, stop=False)
                return pe.matmul(dst, low_w, high_x, start=False, stop=stop)

            def experts(p, step, n):
                if step == "turn2":
                    pe.wait_ge(normed2, p.count(same(1), 1))
                    turn_rows(p, xn2, "Y", 0)
                elif step == "logits":
                    next_use(p, "Y", 1)
                    for t in range(TOK):
                        last = pe.matmul(bank["Y"][:, 8 * t:8 * t + 8], xf[:, t * P:(t + 1) * P], router[:, :],
                                         start=True, stop=True)
                    last.then_inc(filled["Y"], 1)
                elif step == "wturn":
                    pe.wait_ge(routed, p.count(same(1), 1))
                    next_use(p, "Y", 2)
                    for t in range(TOK):
                        last = pe.transpose(bank["Y"][0:8, t * P:(t + 1) * P], wtok[:, 2, t, :], ident)
                    last.then_inc(filled["Y"], 1)
                elif step == "begin":
                    pe.wait_ge(xl_ready, p.count(same(1), 1))
                    if p.kind == "A":
                        pe.wait_ge(pieces_cut, 2 * PIECES)
                elif step == "gate":
                    if n == 0:
                        pe.wait_ge(a_ready, p.count(same(FT), 0))
                    else:
                        pe.wait_ge(h_ready, p.count(same(FT), n - 1))
                    c = slice(n * P, (n + 1) * P)
                    product(product_bank(2 * n)[:, :], w_hi[0][:, c], w_lo[0][:, c], xh[:, :], xl[:, :]
                            ).then_inc(gate_done, 1)
                elif step == "up":
                    if n == 0:
                        pe.wait_ge(h_ready, p.count(same(FT), 0))
                    else:
                        pe.wait_ge(a_ready, p.count(same(FT), n))
                    c = slice(n * P, (n + 1) * P)
                    product(product_bank(2 * n + 1)[:, :], w_hi[1][:, c], w_lo[1][:, c], xh[:, :], xl[:, :]
                            ).then_inc(up_done, 1)
                elif step == "down":
                    pe.wait_ge(hl_ready, p.count(same(FT), n + 1))
                    if n == 0:
                        pe.wait_ge(emptied["Y"], use(p, "Y", 2))
                    c = slice(n * P, (n + 1) * P)
                    product(bank["Y"][:, :], wd_hi[:, c], wd_lo[:, c], hid_hi[:, n % CUT_RING, :],
                            hid_lo[:, n % CUT_RING, :], start=(n == 0), stop=(n == FT - 1)).then_inc(down_done, 1)
                elif step == "end":
                    pe.wait_ge(summed, p.count(same(1), 1))
                    for t in range(TOK):
                        last = pe.transpose(bank["Y"][:, t * P:(t + 1) * P], total[:, t * P:(t + 1) * P], ident)
                    last.then_inc(filled["Y"], 1)

            run_passes(pe, "pe", attention, experts)


def kernel(**inputs):
    import concourse.bacc as bacc
    from concourse.bass_utils import run_bass_kernel_spmd

    def a(name):
        return np.asarray(inputs["L0_" + name])

    w_b = a("attn_b_qkv_proj").reshape(P, 3, D).transpose(2, 1, 0)
    b_b = a("attn_b_qkv_bias").reshape(P, 3)
    inner = lambda shared, routed: np.concatenate([shared[None], routed]).reshape(-1, D)
    arrays = {
        "x": a("attn_a_hidden_states").reshape(BATCH * SEQ, D),
        "w_qk": np.stack([np.stack([a("attn_a_Wq"), a("attn_a_Wk")], 1), w_b[:, 0:2]], 1),
        "b_qk": np.stack([np.stack([a("attn_a_bq"), a("attn_a_bk")], 1), b_b[:, 0:2]], 1),
        "w_vvo": np.stack([a("attn_a_Wv"), w_b[:, 2], a("attn_b_out_proj").T], 1),
        "b_rows": np.concatenate([a("attn_a_bv"), b_b[:, 2], a("attn_b_out_bias"), a("ffn_rb")]).reshape(1, -1),
        "rel": a("attn_a_rel_bias"),
        "wg": inner(a("ffn_sg"), a("ffn_rg")).T, "wu": inner(a("ffn_su"), a("ffn_ru")).T,
        "wd": inner(a("ffn_sd").T, a("ffn_rd").transpose(0, 2, 1)),
        "wr": a("ffn_wr").T, "const": constants(),
    }
    arrays = {f"in_{k}": np.ascontiguousarray(v) for k, v in arrays.items()}
    nc = bacc.Bacc("TRN2", target_bir_lowering=False, num_devices=1)
    args = [nc.dram_tensor(k, v.shape, mybir.dt.from_np(v.dtype), kind="ExternalInput").ap() for k, v in arrays.items()]
    out = nc.dram_tensor("out_x", (BATCH * SEQ, D), F32, kind="ExternalOutput").ap()
    program(nc, *args, out)
    result = run_bass_kernel_spmd(nc, [arrays], core_ids=[0])
    return result.results[0]["out_x"].reshape(BATCH, SEQ, D)
```
